# Optimizing a Trainium2 kernel written in Bass

```python
import numpy as np
import jax
import jax.numpy as jnp

def _softmax(x, axis=-1):
    return jax.nn.softmax(x, axis=axis)

def _gelu(x):
    return jax.nn.gelu(x, approximate=True)

def _silu(x):
    return jax.nn.silu(x)

def _sigmoid(x):
    return jax.nn.sigmoid(x)

def _layernorm(x, axis=-1, eps=1e-05):
    m = jnp.mean(x, axis=axis, keepdims=True)
    v = jnp.var(x, axis=axis, keepdims=True)
    return (x - m) / jnp.sqrt(v + eps)

def _scatter_add(tgt, idx, src, axis=0):
    return tgt.at[idx].add(src)

def _segment_sum(src, seg, n):
    return jax.ops.segment_sum(src, seg, n)
kernel_name = 'mk_decoder_preln_d1_seqx_r8_3d5442'

def setup_inputs(seed: int=0):
    np.random.seed(seed)
    _w = jnp.asarray

    def _rec_inputs():
        import jax
        import jax.numpy as jnp
        _rk = jax.random.key(seed)
        x = -0.0003929 + 0.9999 * jax.random.normal(jax.random.fold_in(_rk, 1), (4, 256, 256), jnp.float32)
        _lenS = 256 - jax.random.randint(jax.random.fold_in(_rk, 7), (4,), 0, max(1, 256 // 4) + 1, jnp.int32)
        _lenS2 = 64 - jax.random.randint(jax.random.fold_in(_rk, 8), (4,), 0, max(1, 64 // 4) + 1, jnp.int32)
        _ctx_2048P = jax.random.normal(jax.random.fold_in(_rk, 11), (4, 16, 256), jnp.float32)
        _ctx_2048c = jax.random.dirichlet(jax.random.fold_in(_rk, 511), 0.3 * jnp.ones((16,), jnp.float32), (4, 64))
        _ctx_2048t = jnp.einsum('bsk,bkd->bsd', _ctx_2048c, _ctx_2048P)
        _ctx_2048t = _ctx_2048t * jax.lax.rsqrt(jnp.mean(jnp.square(_ctx_2048t)) + 1e-12) * 0.953939
        ctx_2048 = -1.39393e-06 + 0.999914 * (_ctx_2048t + 0.3 * jax.random.normal(jax.random.fold_in(_rk, 611), (4, 64, 256), jnp.float32))
        itok_BxS_0_1023 = jax.random.randint(jax.random.fold_in(_rk, 12), (4, 256), 0, 128, jnp.int32)
        return (x, ctx_2048, itok_BxS_0_1023)
    x, ctx_2048, itok_BxS_0_1023 = _rec_inputs()

    def _L0_attn_setup():
        import jax, jax.numpy as jnp
        import numpy as np
        EPS = 1e-05

        def _quant_weight(w):
            scale = jnp.mean(jnp.abs(w)) + EPS
            wq = jnp.clip(jnp.round(w / scale), -1.0, 1.0) * scale
            return wq

        def _quant_act(x):
            s = 127.0 / (jnp.max(jnp.abs(x), axis=-1, keepdims=True) + EPS)
            xq = jnp.clip(jnp.round(x * s), -128.0, 127.0) / s
            return xq
        key = jax.random.key(seed)
        kx, kw = jax.random.split(key)
        B, S, H, L = (4, 256, 256, 8)
        x = jax.random.normal(kx, (B, S, H), dtype=jnp.float32)
        W = jax.random.normal(kw, (L, H, H), dtype=jnp.float32) * 0.02
        return {'x': x, 'W': W}
    _L0_attn_all = _L0_attn_setup()
    _L0_attn_in = {k: v for k, v in _L0_attn_all.items() if k in ('W',)}
    del _L0_attn_all

    def _L0_xattn_setup():
        import jax, jax.numpy as jnp
        import numpy as np
        B, Lq, Lk = (2, 512, 128)
        Q_DIM, KV_DIM = (256, 256)
        H, HD = (16, 128)
        KVC, QC, R = (64, 96, 64)
        LOOKBACK = 8
        NEG = -1e+30

        def _rope(x, L):
            half = x.shape[-1] // 2
            inv_freq = 1.0 / 10000.0 ** (jnp.arange(half, dtype=jnp.float32) / half)
            ang = jnp.arange(L, dtype=jnp.float32)[:, None] * inv_freq
            cos, sin = (jnp.cos(ang), jnp.sin(ang))
            x1, x2 = (x[..., :half], x[..., half:])
            return jnp.concatenate([x1 * cos - x2 * sin, x1 * sin + x2 * cos], axis=-1)
        key = jax.random.key(seed)
        ks = jax.random.split(key, 11)

        def w(k, shape, fan_in):
            return jax.random.normal(k, shape, jnp.float32) / np.sqrt(fan_in).astype(np.float32)
        return {'q': jax.random.normal(ks[0], (B, Lq, Q_DIM), jnp.float32), 'kv': jax.random.normal(ks[1], (B, Lk, KV_DIM), jnp.float32), 'seg_id': jnp.sort(jax.random.randint(ks[2], (B, Lq), 0, Lk), axis=-1), 'W_kvc': w(ks[3], (KV_DIM, KVC), KV_DIM), 'W_dq': w(ks[4], (Q_DIM, QC), Q_DIM), 'W_uq': w(ks[5], (QC, H * HD), QC), 'W_qr': w(ks[6], (QC, H * R), QC), 'W_uk': w(ks[7], (KVC, H * HD), KVC), 'W_kr': w(ks[8], (KVC, R), KVC), 'W_uv': w(ks[9], (KVC, H * HD), KVC), 'W_o': w(ks[10], (H * HD, Q_DIM), H * HD)}
    _L0_xattn_all = _L0_xattn_setup()
    _L0_xattn_in = {k: v for k, v in _L0_xattn_all.items() if k in ('W_kvc', 'W_dq', 'W_uq', 'W_qr', 'W_uk', 'W_kr', 'W_uv', 'W_o')}
    del _L0_xattn_all

    def _L0_ffn_setup():
        import jax, jax.numpy as jnp
        import numpy as np
        EPS = 1e-08

        def _quantize(w):
            gamma = jnp.mean(jnp.abs(w))
            return jnp.clip(jnp.round(w / (gamma + EPS)), -1.0, 1.0)

        def _bitlinear(x, w):
            return jnp.matmul(x, _quantize(w).T)
        key = jax.random.key(seed)
        k1, k2, k3, k4 = jax.random.split(key, 4)
        d, h = (256, 704)
        x = jax.random.normal(k1, (4, 256, d), dtype=jnp.float32)
        w1 = jax.random.normal(k2, (h, d), dtype=jnp.float32)
        w2 = jax.random.normal(k3, (h, d), dtype=jnp.float32)
        w3 = jax.random.normal(k4, (d, h), dtype=jnp.float32)
        return {'x': x, 'w1': w1, 'w2': w2, 'w3': w3}
    _L0_ffn_all = _L0_ffn_setup()
    _L0_ffn_in = {k: v for k, v in _L0_ffn_all.items() if k in ('w1', 'w2', 'w3')}
    del _L0_ffn_all
    return {'x': x, 'ctx_2048': ctx_2048, 'itok_BxS_0_1023': itok_BxS_0_1023, 'L0_attn_W': _L0_attn_in['W'], 'L0_xattn_W_kvc': _L0_xattn_in['W_kvc'], 'L0_xattn_W_dq': _L0_xattn_in['W_dq'], 'L0_xattn_W_uq': _L0_xattn_in['W_uq'], 'L0_xattn_W_qr': _L0_xattn_in['W_qr'], 'L0_xattn_W_uk': _L0_xattn_in['W_uk'], 'L0_xattn_W_kr': _L0_xattn_in['W_kr'], 'L0_xattn_W_uv': _L0_xattn_in['W_uv'], 'L0_xattn_W_o': _L0_xattn_in['W_o'], 'L0_ffn_w1': _L0_ffn_in['w1'], 'L0_ffn_w2': _L0_ffn_in['w2'], 'L0_ffn_w3': _L0_ffn_in['w3']}

def reference(x, ctx_2048, itok_BxS_0_1023, L0_attn_W, L0_xattn_W_kvc, L0_xattn_W_dq, L0_xattn_W_uq, L0_xattn_W_qr, L0_xattn_W_uk, L0_xattn_W_kr, L0_xattn_W_uv, L0_xattn_W_o, L0_ffn_w1, L0_ffn_w2, L0_ffn_w3):
    import jax
    import jax.numpy as jnp

    def _L0_attn_ref(x, W):
        import jax, jax.numpy as jnp
        import numpy as np
        EPS = 1e-05

        def _quant_weight(w):
            scale = jnp.mean(jnp.abs(w)) + EPS
            wq = jnp.clip(jnp.round(w / scale), -1.0, 1.0) * scale
            return wq

        def _quant_act(x):
            s = 127.0 / (jnp.max(jnp.abs(x), axis=-1, keepdims=True) + EPS)
            xq = jnp.clip(jnp.round(x * s), -128.0, 127.0) / s
            return xq

        def layer(h, w):
            hq = _quant_act(h)
            wq = _quant_weight(w)
            out = jnp.einsum('bsh,oh->bso', hq, wq)
            return (out, None)
        y, _ = jax.lax.scan(layer, x, W)
        return y

    def _L0_xattn_ref(q, kv, seg_id, W_kvc, W_dq, W_uq, W_qr, W_uk, W_kr, W_uv, W_o):
        import jax, jax.numpy as jnp
        import numpy as np
        B, Lq, Lk = (2, 512, 128)
        Q_DIM, KV_DIM = (256, 256)
        H, HD = (16, 128)
        KVC, QC, R = (64, 96, 64)
        LOOKBACK = 8
        NEG = -1e+30

        def _rope(x, L):
            half = x.shape[-1] // 2
            inv_freq = 1.0 / 10000.0 ** (jnp.arange(half, dtype=jnp.float32) / half)
            ang = jnp.arange(L, dtype=jnp.float32)[:, None] * inv_freq
            cos, sin = (jnp.cos(ang), jnp.sin(ang))
            x1, x2 = (x[..., :half], x[..., half:])
            return jnp.concatenate([x1 * cos - x2 * sin, x1 * sin + x2 * cos], axis=-1)
        b, lq, _ = q.shape
        lk = kv.shape[1]
        kv_c = kv @ W_kvc
        q_c = q @ W_dq
        q_nope = (q_c @ W_uq).reshape(b, lq, H, HD).transpose(0, 2, 1, 3)
        q_rope = (q_c @ W_qr).reshape(b, lq, H, R).transpose(0, 2, 1, 3)
        k_nope = (kv_c @ W_uk).reshape(b, lk, H, HD)
        v = (kv_c @ W_uv).reshape(b, lk, H, HD)
        k_rope = kv_c @ W_kr
        q_rope = _rope(q_rope, lq)
        k_rope = _rope(k_rope, lk)
        scale = 1.0 / np.sqrt(HD + R).astype(np.float32)
        scores = (jnp.einsum('bhqd,bkhd->bhqk', q_nope, k_nope) + jnp.einsum('bhqr,bkr->bhqk', q_rope, k_rope)) * scale
        k_ids = jnp.arange(lk)[None, None, :]
        qs = seg_id[:, :, None]
        good = (k_ids <= qs) & (k_ids >= qs - LOOKBACK)
        scores = jnp.where(good[:, None, :, :], scores, NEG)
        attn = jax.nn.softmax(scores, axis=-1)
        out = jnp.einsum('bhqk,bkhd->bqhd', attn, v).reshape(b, lq, H * HD)
        return out @ W_o

    def _L0_ffn_ref(x, w1, w2, w3):
        import jax, jax.numpy as jnp
        import numpy as np
        EPS = 1e-08

        def _quantize(w):
            gamma = jnp.mean(jnp.abs(w))
            return jnp.clip(jnp.round(w / (gamma + EPS)), -1.0, 1.0)

        def _bitlinear(x, w):
            return jnp.matmul(x, _quantize(w).T)
        x1 = _bitlinear(x, w1)
        x2 = _bitlinear(x, w2)
        hidden = jax.nn.sigmoid(x1) * x2
        return _bitlinear(hidden, w3)
    x = x + _L0_attn_ref(_layernorm(x, axis=-1), L0_attn_W)
    x = x + _L0_xattn_ref(_layernorm(x, axis=-1), ctx_2048, itok_BxS_0_1023, L0_xattn_W_kvc, L0_xattn_W_dq, L0_xattn_W_uq, L0_xattn_W_qr, L0_xattn_W_uk, L0_xattn_W_kr, L0_xattn_W_uv, L0_xattn_W_o)
    x = x + _L0_ffn_ref(_layernorm(x, axis=-1), L0_ffn_w1, L0_ffn_w2, L0_ffn_w3)
    return x

_drawn_inputs = setup_inputs


def setup_inputs(seed=0):
    import zlib

    import numpy as np

    out = dict(_drawn_inputs(seed))
    spreads = {}
    factors = {'L0_attn_W': 8.0,
     'ctx_2048': 4.078,
     'L0_xattn_W_kvc': 3.867,
     'L0_xattn_W_dq': 8.0,
     'L0_xattn_W_uq': 8.0,
     'L0_xattn_W_qr': 8.0,
     'L0_xattn_W_uk': 8.0,
     'L0_xattn_W_kr': 8.0,
     'L0_xattn_W_uv': 3.886,
     'L0_xattn_W_o': 3.866}
    for name, (base, spread) in spreads.items():
        noise = np.random.default_rng([zlib.crc32(name.encode()), seed]).standard_normal(out[name].shape)
        drawn = base * np.exp(spread * noise) if base else spread * noise
        out[name] = jnp.asarray(drawn.astype(out[name].dtype))
    for name, factor in factors.items():
        out[name] = (out[name] * factor).astype(out[name].dtype)
    return out
```

```python
from contextlib import ExitStack

import numpy as np

import concourse.bass as bass
from concourse import mybir

F32 = mybir.dt.float32
F16 = mybir.dt.float16
BF16 = mybir.dt.bfloat16
I32 = mybir.dt.int32
U32 = mybir.dt.uint32
ALU = mybir.AluOpType
ACT = mybir.ActivationFunctionType
AX = mybir.AxisListType

P = 128
B, S, D = 4, 256, 256
T = B * S
NT = T // P
KD = D // P
L = 8
LK = 64
H, HD, R = 16, 128, 64
QC, KVC = 96, 64
LOOKBACK = 8
F = 704
FJ = (F + P - 1) // P
NEG = -1e30
LN_EPS = 1e-5
Q_EPS = 1e-5
MAGIC = 1.5 * 2.0**23


def build(nc, x, w_attn, ident16, ident32, ctxT, seg, w_kvc, w_dq, w_uqT, w_qr, w_uk, w_kr, w_uv, w_o, w12, w3, rope_q, rope_k,
          key_index, neg_eye, out):
    with ExitStack() as ctx:
        def sb(name, shape, dt):
            return ctx.enter_context(nc.sbuf_tensor(name, shape, dt))

        def ps(name, shape, dt):
            return ctx.enter_context(nc.psum_tensor(name, shape, dt))

        def sem(name):
            return ctx.enter_context(nc.semaphore(name))

        xs = sb("xs", [P, NT, D], F32)
        arena_a = sb("arena_a", [P, L * KD * D], F32)
        arena_o = sb("arena_o", [P, H * D], F32)
        arena_u = sb("arena_u", [P, 2 * H * HD], F32)
        wa = arena_a[:, :].rearrange("p (l c) -> p l c", l=L)
        t1 = arena_a[:, 0:H // 2 * S].rearrange("p (h s) -> p h s", h=H // 2)
        t2 = arena_a[:, H // 2 * S:H * S].rearrange("p (h s) -> p h s", h=H // 2)
        wo = arena_o[:, :].rearrange("p (h d) -> p h d", h=H)
        hid16 = arena_o[:, 0:FJ * 512].bitcast(F16).rearrange("p (n j t) -> p n j t", n=2, j=FJ)
        wuk = arena_u[0:KVC, 0:H * HD]
        wuv = arena_u[0:KVC, H * HD:2 * H * HD]
        es = arena_u[:, 0:2 * H * LK].rearrange("p (n h k) -> p n h k", n=2, h=H)
        pT = arena_u[:, 2 * H * LK:4 * H * LK].rearrange("p (n c) -> p n c", n=2)
        arena_k = sb("arena_k", [P, H * QC + 16 * B * LK], F32)
        wkvc = sb("wkvc", [P, KD, KVC], F32)
        wdq = sb("wdq", [P, KD, QC], F32)
        wqr = sb("wqr", [QC, H * R], F32)
        wkr = sb("wkr", [KVC, 2, 2 * R], F32)
        rq = sb("rq", [P, 2, S], F32)
        rk = sb("rk", [P, 4, LK], F32)
        kidx = sb("kidx", [LK, 1], F32)
        negI = sb("negI", [LK, 8 * LK], BF16)
        bad = sb("bad", [LK, T], BF16)
        id32 = sb("id32", [P, P], F32)
        kvc = sb("kvc", [KVC, B * LK], F32)
        kbd = sb("kbd", [P, B, 2, 2 * LK], F32)
        ys = sb("ys", [QC, B, H, LK], F32)
        vn = sb("vn", [P, B, H // 2, D], F32)
        qcT = sb("qcT", [QC, T], F32)
        smax = sb("smax", [P, 2, H], F32)
        ssum = sb("ssum", [P, 2, H], F32)
        srec = sb("srec", [P, 2, H], F32)
        fsum = sb("fsum", [P, 4], F32)
        fsc = sb("fsc", [P, 4], F32)
        fth = sb("fth", [P, 4], F32)
        fthn = sb("fthn", [P, 4], F32)
        ta = sb("ta", [P, L, KD, D], F16)
        tneg = sb("tneg", [P, KD * D], F16)
        id16 = sb("id16", [P, P], F16)
        ones = sb("ones", [P, P], F32)
        mtile = sb("mtile", [P, D], F32)
        wsum = sb("wsum", [P, L], F32)
        wscale = sb("wscale", [P, L], F32)
        wth = sb("wth", [P, L], F32)
        wthn = sb("wthn", [P, L], F32)
        stats = sb("stats", [P, NT, 6], F32)
        mv = sb("mv", [P, NT, 2], F32)
        rstd = sb("rstd", [P, NT], F32)
        rv = sb("rv", [P, NT], F32)
        rt = sb("rt", [P, NT], F32)
        h0 = sb("h0", [P, NT, D], F32)
        mx = sb("mx", [P, NT], F32)
        mh = sb("mh", [P, NT], F32)
        mxe = sb("mxe", [P, NT], F32)
        rc = sb("rc", [P, NT], F32)
        rr = sb("rr", [P, NT], F32)
        ss = sb("ss", [P, NT], F32)
        gg = sb("gg", [P, NT], F32)
        gm = sb("gm", [P, NT], F32)
        sg = sb("sg", [P, NT], F32)
        cs = sb("cs", [P, NT], F32)
        km = sb("km", [P, NT, D], F32)
        kk = sb("kk", [P, NT, D], F16)
        vhi = sb("vhi", [P, NT, D], F16)
        vlo = sb("vlo", [P, NT, D], F16)
        vT = sb("vT", [P, NT, 4 * P], F16)

        def part(arena, start, *dims):
            size = int(np.prod(dims))
            v = arena[:, start:start + size]
            if len(dims) == 2:
                v = v.rearrange("p (a b) -> p a b", a=dims[0])
            return v

        wuqT = part(arena_k, 0, H, QC)
        knT = part(arena_k, H * QC, 4, 2 * B * LK)
        rot = part(arena_k, H * QC + 8 * B * LK, 4, B * LK)
        rawk = part(arena_k, H * QC + 12 * B * LK, 2, B * LK)
        ctxs = part(arena_k, H * QC + 14 * B * LK, KD, B * LK)
        wf = part(arena_k, 0, KD, 2 * F)
        w3s = part(arena_k, KD * 2 * F, FJ, D)
        taf = ta[:, :, :, :].rearrange("p l k d -> p (l k d)")
        wf16 = part(taf, 0, KD, 2 * F)
        kkf = kk[:, :, :].rearrange("p i d -> p (i d)")
        w316 = part(kkf, 0, FJ, D)
        fneg = vlo[:, :, :].rearrange("p i d -> p (i d)")
        vTf = vT[:, :, :].rearrange("p i c -> p (i c)")
        segs = vTf[0:LK, 0:2 * T].bitcast(I32)
        badh = vTf[0:LK, 2 * T:3 * T].bitcast(BF16)
        sgm = part(arena_u, 0, 2, 512)
        hid = part(arena_u, 1024, 2, 512)

        acc = ps("acc", [P, NT, D], F32)
        tp = ps("tp", [P, NT, 4 * P], F16)

        accf = acc[:, :, :].rearrange("p i d -> p (i d)").rearrange("p (b c) -> p b c", b=4)
        tpf = tp[:, :, :].rearrange("p i c -> p (i c)").bitcast(F32).rearrange("p (b c) -> p b c", b=4)

        def bank(n):
            return accf[:, n, :] if n < 4 else tpf[:, n - 4, :]

        x_in = sem("x_in")
        w_in = [sem(f"w_in{l}") for l in range(L)]
        id_in = sem("id_in")
        y_out = sem("y_out")
        k_in = sem("k_in")
        u_in = sem("u_in")
        seg_in = sem("seg_in")
        f_in = sem("f_in")
        mask_ready = sem("mask_ready")
        mask_part = sem("mask_part")
        q_in = sem("q_in")
        prep_done = sem("prep_done")
        prep_read = sem("prep_read")
        rot_in = sem("rot_in")
        kbd_ready = sem("kbd_ready")
        kbd_zero = sem("kbd_zero")
        std2 = sem("std2")
        var2 = sem("var2")
        norm_ready = sem("norm_ready")
        qt_done = sem("qt_done")
        qt_read = sem("qt_read")
        qc_done = sem("qc_done")
        qc_read = sem("qc_read")
        a_done = sem("a_done")
        a_read = sem("a_read")
        s_done = sem("s_done")
        s_read = sem("s_read")
        e_done = sem("e_done")
        r_done = sem("r_done")
        p_done = sem("p_done")
        pt_done = sem("pt_done")
        pt_read = sem("pt_read")
        o_done = sem("o_done")
        x2_done = sem("x2_done")
        fth_ready = sem("fth_ready")
        fabs = sem("fabs")
        ftot = sem("ftot")
        fq = sem("fq")
        norm3 = sem("norm3")
        yhi = sem("yhi")
        ylo = sem("ylo")
        yt_done = sem("yt_done")
        yt_read = sem("yt_read")
        g_done = sem("g_done")
        sig_done = sem("sig_done")
        hid_done = sem("hid_done")
        hhi = sem("hhi")
        hlo = sem("hlo")
        f_done = sem("f_done")
        ones_set = sem("ones_set")
        y_ready = sem("y_ready")
        wabs = sem("wabs")
        wtot = sem("wtot")
        wq = sem("wq")
        var_ready = sem("var_ready")
        std_ready = sem("std_ready")
        dv = sem("dv")
        r_ready = [sem(f"r_ready{g}") for g in range(2)]
        rounded = [sem(f"rounded{g}") for g in range(2)]
        hv = sem("hv")
        g_ready = [sem(f"g_ready{g}") for g in range(2)]
        hi_ready = [sem(f"hi_ready{g}") for g in range(2)]
        lo_ready = [sem(f"lo_ready{g}") for g in range(2)]
        turned = [sem(f"turned{g}") for g in range(2)]
        vt_ready = [sem(f"vt_ready{g}") for g in range(2)]
        acc_ready = [sem(f"acc_ready{g}") for g in range(2)]
        G = 4

        fills = [("kvc", 0), ("rot", 0), ("kn", 0), ("v", 0)]
        for hp in range(H // 2):
            if hp + 1 < H // 2:
                fills += [("kn", hp + 1), ("v", hp + 1)]
            fills += [("y", hp), ("vn", 2 * hp), ("vn", 2 * hp + 1)]
        filled = {f: n + 1 for n, f in enumerate(fills)}
        half = lambda h: slice(LK * (h % 2), LK * (h % 2) + LK)
        qT = km[:, :, :].rearrange("p i d -> p (i d)").rearrange("p (k t) -> p k t", k=KD)
        yT = vT[:, :, :].rearrange("p i c -> p (i c)").rearrange("p (c t) -> p c t", c=2 * KD)
        hid_hl = [hid16, arena_a[:, 0:FJ * 512].bitcast(F16).rearrange("p (n j t) -> p n j t", n=2, j=FJ)]
        SCALE = 1.0 / float(np.sqrt(np.float32(HD + R)))
        CH = 512
        NC = T // CH
        rows = lambda j: min(P, F - j * P)

        block = ctx.enter_context(nc.Block())

        @block.sync
        def _(sp):
            sp.dma_start(xs[:], x.rearrange("(i p) d -> p i d", p=P)).then_inc(x_in, 16)
            sp.dma_start(id16[:], ident16).then_inc(id_in, 16)
            sp.dma_start(ctxs, ctxT).then_inc(k_in, 16)
            sp.dma_start(wkvc[:], w_kvc).then_inc(k_in, 16)
            sp.dma_start(wkr[:], w_kr).then_inc(k_in, 16)
            sp.dma_start(rk[:], rope_k).then_inc(k_in, 16)
            for l in range(L):
                sp.dma_start(wa[:, l, :], w_attn[:, l, :]).then_inc(w_in[l], 16)
            sp.wait_ge(prep_read, len(fills))
            sp.wait_ge(kbd_ready, 1)
            sp.dma_start(wf, w12).then_inc(f_in, 16)
            sp.dma_start(w3s[:, 0:FJ - 1, :], w3[:, 0:FJ - 1, :]).then_inc(f_in, 16)
            sp.dma_start(w3s[0:F - (FJ - 1) * P, FJ - 1, :], w3[0:F - (FJ - 1) * P, FJ - 1, :]).then_inc(f_in, 16)
            for i in range(NT):
                sp.wait_ge(y_ready, i + 1)
                sp.dma_start(out[P * i:P * (i + 1), :], xs[:, i, :]).then_inc(y_out, 16)
            sp.wait_ge(y_out, 16 * NT)

        @block.scalar
        def _(act):
            act.dma_start(wuk, w_uk).then_inc(u_in, 16)
            act.dma_start(wuv, w_uv).then_inc(u_in, 16)
            act.dma_start(wuqT, w_uqT).then_inc(u_in, 16)
            act.dma_start(wo, w_o).then_inc(u_in, 16)
            act.dma_start(segs, seg.partition_broadcast(LK)).then_inc(seg_in, 16)
            act.dma_start(kidx[:], key_index).then_inc(seg_in, 16)
            act.dma_start(wdq[:], w_dq).then_inc(q_in, 16)
            act.dma_start(wqr[:], w_qr).then_inc(q_in, 16)
            act.dma_start(rq[:], rope_q).then_inc(q_in, 16)
            act.dma_start(id32[:], ident32).then_inc(q_in, 16)
            act.dma_start(negI[:], neg_eye).then_inc(q_in, 16)
            act.wait_ge(var_ready, 1)
            nc.scalar.activation(rt[:], rv[:], ACT.Sqrt).then_inc(std_ready, 1)
            for n, (kind, i) in enumerate(fills):
                act.wait_ge(prep_done, n + 1)
                src = bank(4 + n % 4)
                if kind == "kvc":
                    last = nc.scalar.copy(kvc[:], src[0:KVC, 0:B * LK])
                elif kind == "rot":
                    last = nc.scalar.copy(rawk[:, :, :].rearrange("p n c -> p (n c)"), src)
                elif kind == "kn" or kind == "v":
                    last = nc.scalar.copy(knT[:, i % 2 + 2 * (kind == "v"), :], src)
                elif kind == "y":
                    last = nc.scalar.copy(ys[:, :, 2 * i:2 * i + 2, :].rearrange("q b e k -> q e b k"),
                                          src[0:QC, :].rearrange("q (e b k) -> q e b k", e=2, b=B))
                else:
                    for m in range(2):
                        last = nc.scalar.copy(vn[half(i), :, i // 2, :].rearrange("p (n m) d -> p m n d", m=2)[:, m],
                                              src[half(m), :].rearrange("p (n d) -> p n d", n=2))
                last.then_inc(prep_read, 1)

            act.wait_ge(ones_set, 2)

            def round_group(g, q):
                act.wait_ge(r_ready[g], q + 1)
                for i in range(G * g, G * g + G):
                    src = acc if not isinstance(q, int) or q else h0
                    nc.scalar.activation(km[:, i, :], src[:, i, :], ACT.Identity, scale=rr[:, i:i + 1],
                                         bias=mtile[:, 0:1]).then_inc(rounded[g], 1)

            def copy_out(g, q):
                for j in range(2):
                    act.wait_ge(turned[g], 2 * q + j + 1)
                    i = G * g + 2 * j
                    nc.scalar.copy(vT[:, i:i + 2, :].bitcast(U32), tp[:, i:i + 2, :].bitcast(U32)).then_inc(vt_ready[g], 1)

            round_group(0, 0)
            round_group(1, 0)
            copy_out(0, 0)
            with act.Fori(1, L) as q:
                round_group(0, q)
                copy_out(1, q - 1)
                round_group(1, q)
                copy_out(0, q)
            copy_out(1, L - 1)

            act.wait_ge(var2, 1)
            nc.scalar.activation(rt[:], rv[:], ACT.Sqrt).then_inc(std2, 1)
            for j in range(NT // 2):
                act.wait_ge(qt_done, j + 1)
                nc.scalar.copy(qT[:, :, 2 * P * j:2 * P * (j + 1)].rearrange("p k (i t) -> p i k t", i=2),
                               bank(j).rearrange("p (i k t) -> p i k t", i=2, k=KD)).then_inc(qt_read, 1)
            for c in range(2):
                act.wait_ge(qc_done, c + 1)
                nc.scalar.copy(qcT[:, 512 * c:512 * (c + 1)], bank(4 + c)[0:QC, :]).then_inc(qc_read, 1)

            def exps(i):
                act.wait_ge(s_read, i + 1)
                nc.scalar.activation(es[:, i % 2], es[:, i % 2], ACT.Exp, scale=SCALE).then_inc(e_done, 1)

            def copy_probs(i):
                act.wait_ge(pt_done, i + 1)
                nc.scalar.copy(pT[:, i % 2, :], tpf[:, 2:4, :].rearrange("p b c -> p (b c)")).then_inc(pt_read, 1)

            exps(0)
            exps(1)
            for b in range(B):
                copy_probs(2 * b)
                copy_probs(2 * b + 1)
                if b + 1 < B:
                    exps(2 * b + 2)
                    exps(2 * b + 3)
            act.wait_ge(var2, 2)
            nc.scalar.activation(rt[:], rv[:], ACT.Sqrt).then_inc(std2, 1)
            for i in range(NT):
                act.wait_ge(norm3, i + 1)
                nc.scalar.copy(vhi[:, i, :], h0[:, i, :]).then_inc(yhi, 1)
            for j in range(NT // 2):
                act.wait_ge(yt_done, j + 1)
                nc.scalar.copy(yT[:, :, 2 * P * j:2 * P * (j + 1)].bitcast(U32).rearrange("p c (i t) -> p i c t", i=2),
                               tp[:, 2 * j:2 * j + 2, :].bitcast(U32).rearrange("p i (c t) -> p i c t", c=2 * KD)
                               ).then_inc(yt_read, 1)
            for n in range(NC * FJ):
                c, j = divmod(n, FJ)
                r = slice(0, rows(j))
                act.wait_ge(g_done, n + 1)
                if n >= 2:
                    act.wait_ge(hid_done, n - 1)
                nc.scalar.activation(sgm[r, n % 2, :], bank(2 * (n % 2))[r], ACT.Sigmoid, scale=1.0 / 2048).then_inc(sig_done, 1)
                act.wait_ge(hid_done, n + 1)
                nc.scalar.copy(hid_hl[c][r, 0, j, :], hid[r, n % 2, :]).then_inc(hhi, 1)

        @block.gpsimd
        def _(pool):
            nc.gpsimd.memset(ones[:], 1.0).then_inc(ones_set, 1)
            nc.gpsimd.memset(mtile[:], MAGIC).then_inc(ones_set, 1)

            pool.wait_ge(ones_set, 2)

            nc.gpsimd.memset(kbd[:], 0.0).then_inc(kbd_zero, 1)
            pool.wait_ge(k_in, 64)
            pool.wait_ge(prep_read, filled["rot", 0])
            for n, (src, dst) in enumerate(((0, 0), (1, 1), (1, 2), (0, 3))):
                last = nc.gpsimd.tensor_tensor(rot[:, dst, :].rearrange("p (b k) -> p b k", b=B),
                                               rawk[:, src, :].rearrange("p (b k) -> p b k", b=B),
                                               rk[:, dst:dst + 1, :].to_broadcast([P, B, LK]), ALU.mult)
            last.then_inc(rot_in, 1)
            pool.wait_ge(rot_in, 1)
            pool.wait_ge(kbd_zero, 1)
            for n in range(2):
                for e in range(2):
                    last = nc.gpsimd.tensor_tensor(kbd[half(e), :, n, half(e)],
                                                   rot[half(e), 2 * n, :].rearrange("p (b k) -> p b k", b=B),
                                                   rot[half(e), 2 * n + 1, :].rearrange("p (b k) -> p b k", b=B), ALU.add)
            last.then_inc(kbd_ready, 1)
            pool.wait_ge(seg_in, 32)
            nc.gpsimd.tensor_scalar(badh, segs, kidx[:], 0.0, ALU.subtract, ALU.is_lt)
            nc.gpsimd.tensor_scalar(bad[:], segs, kidx[:], float(LOOKBACK), ALU.subtract, ALU.is_gt).then_inc(mask_part, 1)
            pool.wait_ge(mask_part, 1)
            nc.gpsimd.tensor_tensor(bad[:], bad[:], badh, ALU.add).then_inc(mask_ready, 1)

            def hi_group(g, q):
                for j in range(G):
                    i = G * g + j
                    pool.wait_ge(rounded[g], G * q + j + 1)
                    nc.gpsimd.tensor_tensor(kk[:, i, :], km[:, i, :], mtile[:], ALU.subtract).then_inc(hi_ready[g], 1)

            hi_group(0, 0)
            hi_group(1, 0)
            with pool.Fori(1, L) as q:
                hi_group(0, q)
                hi_group(1, q)
            for i in range(NT):
                pool.wait_ge(r_done, i + 1)
                nc.gpsimd.tensor_tensor(es[:, i % 2], es[:, i % 2], srec[:, i % 2, :].unsqueeze(2).to_broadcast([P, H, LK]),
                                        ALU.mult).then_inc(p_done, 1)

        @block.vector
        def _(dve):
            done = [0]

            def link(ins):
                done[0] += 1
                ins.then_inc(dv, 1)
                dve.wait_ge(dv, done[0])

            dve.wait_ge(x_in, 16)
            for i in range(NT):
                last = nc.vector.bn_stats(stats[:, i, :], xs[:, i, :])
            link(last)
            for i in range(NT):
                last = nc.vector.bn_aggr(mv[:, i, :], stats[:, i, :])
            link(last)
            nc.vector.tensor_scalar(rv[:], mv[:, :, 1], LN_EPS, None, ALU.add).then_inc(var_ready, 1)
            for l in range(L):
                dve.wait_ge(w_in[l], 16)
                nc.vector.tensor_reduce(wsum[:, l:l + 1], wa[:, l, :], axis=AX.X, op=ALU.add,
                                        apply_absolute_value=True).then_inc(wabs, 1)
            dve.wait_ge(std_ready, 1)
            dve.wait_ge(var_ready, 1)
            link(nc.vector.reciprocal(rstd[:], rt[:]))
            link(nc.vector.tensor_tensor(rt[:], rstd[:], rstd[:], ALU.mult))
            link(nc.vector.tensor_tensor(rt[:], rt[:], rv[:], ALU.mult))
            link(nc.vector.tensor_scalar(rt[:], rt[:], -0.5, 1.5, ALU.mult, ALU.add))
            link(nc.vector.tensor_tensor(rstd[:], rstd[:], rt[:], ALU.mult))
            for i in range(NT):
                last = nc.vector.tensor_scalar(h0[:, i, :], xs[:, i, :], mv[:, i, 0:1], rstd[:, i:i + 1],
                                               ALU.subtract, ALU.mult)
            link(last)
            link(nc.vector.tensor_reduce(mx[:], h0[:], axis=AX.X, op=ALU.max, apply_absolute_value=True))
            dve.wait_ge(wtot, 1)
            link(nc.vector.tensor_scalar(wscale[:], acc[:, 0, 0:L], 1.0 / (D * D), Q_EPS, ALU.mult, ALU.add))
            nc.vector.tensor_scalar(wth[:], wscale[:], 0.5, None, ALU.mult)
            link(nc.vector.tensor_scalar(wthn[:], wscale[:], -0.5, None, ALU.mult))
            link(nc.vector.tensor_scalar(mxe[:], mx[:], Q_EPS, None, ALU.add))
            link(nc.vector.reciprocal(rc[:], mxe[:]))
            for g in range(2):
                s = slice(G * g, G * g + G)
                nc.vector.tensor_scalar(rr[:, s], rc[:, s], 127.0, None, ALU.mult).then_inc(r_ready[g], 1)
            for g in range(2):
                dve.wait_ge(r_ready[g], 1)
            link(nc.vector.reciprocal(gg[:], rr[:]))
            for g in range(2):
                s = slice(G * g, G * g + G)
                nc.vector.tensor_scalar(gm[:, s].bitcast(I32), gg[:, s].bitcast(I32), 0x7FFFFF, 0x43000000,
                                        ALU.bitwise_and, ALU.bitwise_or).then_inc(g_ready[g], 1)
            link(nc.vector.tensor_scalar(sg[:].bitcast(I32), gg[:].bitcast(I32), 0x7F800000, None, ALU.bitwise_and))
            link(nc.vector.tensor_scalar(cs[:], sg[:], 1.0 / 128.0, wscale[:, 0:1], ALU.mult, ALU.mult))
            for l in range(L):
                link(nc.vector.tensor_scalar(tneg[:], wa[:, l, :], wthn[:, l:l + 1], None, ALU.is_lt))
                nc.vector.scalar_tensor_tensor(ta[:, l].rearrange("p k d -> p (k d)"), wa[:, l, :], wth[:, l:l + 1],
                                               tneg[:], ALU.is_gt, ALU.subtract).then_inc(wq, 1)
                dve.wait_ge(wq, l + 1)

            def lo_tile(g, q, j):
                i = G * g + j
                dve.wait_ge(hi_ready[g], G * q + j + 1)
                nc.vector.tensor_scalar(vhi[:, i, :], kk[:, i, :], gm[:, i:i + 1], None,
                                        ALU.mult).then_inc(hv, 1)
                dve.wait_ge(hv, NT * q + G * g + j + 1)
                nc.vector.scalar_tensor_tensor(vlo[:, i, :], kk[:, i, :], gm[:, i:i + 1], vhi[:, i, :],
                                               ALU.mult, ALU.subtract).then_inc(lo_ready[g], 1)

            base = done[0]
            STEPS = 8

            def scales(g, q, fill):
                s = slice(G * g, G * g + G)
                start = base + STEPS * (2 * (q - 1) + g)
                at = [0]

                def step(ins, filler=None):
                    at[0] += 1
                    ins.then_inc(dv, 1)
                    if filler is not None:
                        fill(filler)
                    dve.wait_ge(dv, start + at[0])

                dve.wait_ge(acc_ready[g], q)
                nc.vector.tensor_reduce(mx[:, G * g:G * g + 2], acc[:, G * g:G * g + 2, :], axis=AX.X, op=ALU.max,
                                        apply_absolute_value=True)
                step(nc.vector.tensor_reduce(mx[:, G * g + 2:G * g + 4], acc[:, G * g + 2:G * g + 4, :], axis=AX.X,
                                             op=ALU.max, apply_absolute_value=True), 0)
                step(nc.vector.tensor_tensor(mh[:, s], mx[:, s], cs[:, s], ALU.mult), 1)
                step(nc.vector.tensor_scalar(mxe[:, s], mh[:, s], Q_EPS, None, ALU.add), 2)
                step(nc.vector.reciprocal(rc[:, s], mxe[:, s]), 3)
                step(nc.vector.tensor_scalar(ss[:, s], rc[:, s], 127.0, None, ALU.mult))
                nc.vector.tensor_tensor(rr[:, s], ss[:, s], cs[:, s], ALU.mult).then_inc(r_ready[g], 1)
                step(nc.vector.reciprocal(gg[:, s], ss[:, s]))
                nc.vector.tensor_scalar(gm[:, s].bitcast(I32), gg[:, s].bitcast(I32), 0x7FFFFF, 0x43000000,
                                        ALU.bitwise_and, ALU.bitwise_or).then_inc(g_ready[g], 1)
                step(nc.vector.tensor_scalar(sg[:, s].bitcast(I32), gg[:, s].bitcast(I32), 0x7F800000, None,
                                             ALU.bitwise_and))
                step(nc.vector.tensor_scalar(cs[:, s], sg[:, s], 1.0 / 128.0, wscale[:, bass.ds(q, 1)], ALU.mult,
                                             ALU.mult))

            for j in range(G):
                lo_tile(0, 0, j)
            with dve.Fori(1, L) as q:
                scales(0, q, lambda j: lo_tile(1, q - 1, j))
                scales(1, q, lambda j: lo_tile(0, q, j))
            for j in range(G):
                lo_tile(1, L - 1, j)
            done[0] = base + STEPS * 2 * (L - 1)

            def norm_scales(n, times):
                for i in range(NT):
                    last = nc.vector.bn_stats(stats[:, i, :], xs[:, i, :])
                link(last)
                for i in range(NT):
                    last = nc.vector.bn_aggr(mv[:, i, :], stats[:, i, :])
                link(last)
                nc.vector.tensor_scalar(rv[:], mv[:, :, 1], LN_EPS, None, ALU.add).then_inc(var2, 1)
                dve.wait_ge(std2, n)
                dve.wait_ge(var2, n)
                link(nc.vector.reciprocal(rstd[:], rt[:]))
                link(nc.vector.tensor_tensor(rt[:], rstd[:], rstd[:], ALU.mult))
                link(nc.vector.tensor_tensor(rt[:], rt[:], rv[:], ALU.mult))
                link(nc.vector.tensor_scalar(rt[:], rt[:], -0.5 * times, 1.5 * times, ALU.mult, ALU.add))
                link(nc.vector.tensor_tensor(rstd[:], rstd[:], rt[:], ALU.mult))

            for g in range(2):
                dve.wait_ge(acc_ready[g], L)
                for i in range(G * g, G * g + G):
                    last = nc.vector.scalar_tensor_tensor(xs[:, i, :], acc[:, i, :], cs[:, i:i + 1], xs[:, i, :],
                                                          ALU.mult, ALU.add)
            link(last)
            norm_scales(1, 1.0)
            for i in range(NT):
                nc.vector.tensor_scalar(h0[:, i, :], xs[:, i, :], mv[:, i, 0:1], rstd[:, i:i + 1],
                                        ALU.subtract, ALU.mult).then_inc(norm_ready, 1)
            dve.wait_ge(f_in, 48)
            link(nc.vector.memset(fsum[:], 0.0))
            for n in range(2):
                nc.vector.tensor_reduce(fsum[:, n:n + 1], wf[:, :, F * n:F * n + F], axis=AX.XY, op=ALU.add,
                                        apply_absolute_value=True)
            nc.vector.tensor_reduce(fsum[:, 2:3], w3s[:, 0:FJ - 1, :], axis=AX.XY, op=ALU.add, apply_absolute_value=True)
            nc.vector.tensor_reduce(fsum[0:rows(FJ - 1), 3:4], w3s[0:rows(FJ - 1), FJ - 1, :], axis=AX.X, op=ALU.add,
                                    apply_absolute_value=True).then_inc(fabs, 1)

            def turn(b):
                for n in range(4):
                    turn_fill(b, n)

            def turn_fill(b, n):
                dve.wait_ge(a_done, 4 * b + n + 1)
                if b > 0 and n == 0:
                    dve.wait_ge(s_done, 2 * b)
                src = bank(0).rearrange("p (h s) -> p h s", h=2)
                nc.vector.tensor_tensor(t1[:, 2 * n:2 * n + 2, :], src, rq[:, 0:1, :].to_broadcast([P, 2, S]), ALU.mult)
                nc.vector.tensor_tensor(t2[:, 2 * n:2 * n + 2, :], src, rq[:, 1:2, :].to_broadcast([P, 2, S]),
                                        ALU.mult).then_inc(a_read, 1)

            def less_max(i):
                src = (accf[:, 2:4, :] if i % 2 == 0 else tpf[:, 0:2, :]).rearrange("p b (h k) -> p (b h) k", k=LK)
                dve.wait_ge(s_done, i + 1)
                if i >= 2:
                    dve.wait_ge(pt_done, i - 1)
                link(nc.vector.tensor_reduce(smax[:, i % 2, :], src, axis=AX.X, op=ALU.max))
                nc.vector.tensor_tensor(es[:, i % 2], src, smax[:, i % 2, :].unsqueeze(2).to_broadcast([P, H, LK]),
                                        ALU.subtract).then_inc(s_read, 1)

            def sums(i):
                dve.wait_ge(e_done, i + 1)
                link(nc.vector.tensor_reduce(ssum[:, i % 2, :], es[:, i % 2], axis=AX.X, op=ALU.add))
                nc.vector.reciprocal(srec[:, i % 2, :], ssum[:, i % 2, :]).then_inc(r_done, 1)

            def add_attn(i):
                dve.wait_ge(o_done, i + 1)
                nc.vector.tensor_tensor(xs[:, i, :], bank(1)[:, 0:D], xs[:, i, :], ALU.add).then_inc(x2_done, 1)

            dve.wait_ge(q_in, 80)
            turn(0)
            for i in range(2):
                less_max(i)
            for i in range(2):
                sums(i)
            dve.wait_ge(ftot, 1)
            link(nc.vector.tensor_scalar(fsc[:, 0:2], bank(1)[:, 0:2], 1.0 / (F * D), 1e-8, ALU.mult, ALU.add))
            link(nc.vector.tensor_reduce(fsum[:, 0:1], bank(1)[:, 2:4], axis=AX.X, op=ALU.add))
            link(nc.vector.tensor_scalar(fsc[:, 2:3], fsum[:, 0:1], 1.0 / (F * D), 1e-8, ALU.mult, ALU.add))
            nc.vector.tensor_scalar(fth[:, 0:3], fsc[:, 0:3], 0.5, None, ALU.mult)
            nc.vector.tensor_scalar(fthn[:, 0:3], fsc[:, 0:3], -0.5, None, ALU.mult).then_inc(fth_ready, 1)
            dve.wait_ge(fth_ready, 1)

            def ternary(n):
                if n < 2 * KD:
                    k, m = divmod(n, 2)
                    w, o, th = wf[:, k, F * m:F * m + F], wf16[:, k, F * m:F * m + F], m
                    tmp = fneg[:, 0:F]
                elif n == 2 * KD:
                    w, o, th = w3s[:, 0:FJ - 1, :], w316[:, 0:FJ - 1, :], 2
                    tmp = fneg[:, 0:(FJ - 1) * D].rearrange("p (j d) -> p j d", j=FJ - 1)
                else:
                    r = slice(0, rows(FJ - 1))
                    w, o, th = w3s[r, FJ - 1, :], w316[r, FJ - 1, :], 2
                    tmp = fneg[r, 0:D]
                q = slice(0, w.shape[0])
                link(nc.vector.tensor_scalar(tmp, w, fthn[q, th:th + 1], None, ALU.is_lt))
                link(nc.vector.scalar_tensor_tensor(o, w, fth[q, th:th + 1], tmp, ALU.is_gt, ALU.subtract))

            for b in range(B):
                for e in range(2):
                    if b + 1 < B:
                        turn_fill(b + 1, 2 * e)
                        turn_fill(b + 1, 2 * e + 1)
                    add_attn(2 * b + e)
                if b < 3:
                    ternary(2 * b)
                    ternary(2 * b + 1)
                if b + 1 < B:
                    for i in (2 * b + 2, 2 * b + 3):
                        less_max(i)
                    for i in (2 * b + 2, 2 * b + 3):
                        sums(i)
            dve.wait_ge(x2_done, NT)
            norm_scales(2, 2048.0)
            for i in range(NT):
                nc.vector.tensor_scalar(h0[:, i, :], xs[:, i, :], mv[:, i, 0:1], rstd[:, i:i + 1],
                                        ALU.subtract, ALU.mult).then_inc(norm3, 1)
            for i in range(NT):
                dve.wait_ge(yhi, i + 1)
                nc.vector.tensor_tensor(vlo[:, i, :], h0[:, i, :], vhi[:, i, :], ALU.subtract).then_inc(ylo, 1)

            def low(n):
                c, j = divmod(n, FJ)
                r = slice(0, rows(j))
                dve.wait_ge(hhi, n + 1)
                nc.vector.tensor_tensor(hid_hl[c][r, 1, j, :], hid[r, n % 2, :], hid_hl[c][r, 0, j, :],
                                        ALU.subtract).then_inc(hlo, 1)

            for n in range(NC * FJ):
                c, j = divmod(n, FJ)
                r = slice(0, rows(j))
                dve.wait_ge(sig_done, n + 1)
                if n >= 2:
                    dve.wait_ge(hlo, n - 1)
                nc.vector.scalar_tensor_tensor(hid[r, n % 2, :], bank(2 * (n % 2) + 1)[r], 1.0 / 16, sgm[r, n % 2, :],
                                               ALU.mult, ALU.mult).then_inc(hid_done, 1)
                if n >= 1:
                    low(n - 1)
            low(NC * FJ - 1)
            for i in range(NT):
                if i % 2 == 0:
                    dve.wait_ge(f_done, i + 2)
                nc.vector.scalar_tensor_tensor(xs[:, i, :], tpf[:, i // 2, (i % 2) * D:(i % 2) * D + D], 1.0 / 128,
                                               xs[:, i, :], ALU.mult, ALU.add).then_inc(y_ready, 1)

        @block.tensor
        def _(pe):
            for n, (kind, i) in enumerate(fills):
                if n >= 4:
                    pe.wait_ge(prep_read, n - 3)
                dst = bank(4 + n % 4)
                if kind == "kvc":
                    pe.wait_ge(k_in, 64)
                    for k in range(KD):
                        last = nc.tensor.matmul(dst[0:KVC, 0:B * LK], wkvc[:, k, :], ctxs[:, k, :], start=k == 0, stop=k == KD - 1)
                elif kind == "rot":
                    pe.wait_ge(prep_read, filled["kvc", 0])
                    for m in range(2):
                        last = nc.tensor.matmul(dst[:, B * LK * m:B * LK * (m + 1)], wkr[:, m, :], kvc[:], start=True, stop=True)
                elif kind in ("kn", "v"):
                    if (kind, i) == ("kn", 0):
                        pe.wait_ge(u_in, 64)
                    w = wuk if kind == "kn" else wuv
                    for e in range(2):
                        h = 2 * i + e
                        last = nc.tensor.matmul(dst[:, B * LK * e:B * LK * (e + 1)], w[:, HD * h:HD * (h + 1)], kvc[:],
                                                start=True, stop=True)
                elif kind == "y":
                    pe.wait_ge(prep_read, filled["kn", i])
                    for e in range(2):
                        last = nc.tensor.matmul(dst[0:QC, B * LK * e:B * LK * (e + 1)], wuqT[:, 2 * i + e, :],
                                                knT[:, i % 2, B * LK * e:B * LK * (e + 1)], start=True, stop=True)
                else:
                    pe.wait_ge(prep_read, filled["v", i // 2])
                    for m in range(2):
                        o = B * LK * (i % 2) + 2 * LK * m
                        last = nc.tensor.matmul(dst[:, D * m:D * (m + 1)], knT[:, 2 + i // 2 % 2, o:o + 2 * LK], wo[:, i, :],
                                                start=True, stop=True)
                last.then_inc(prep_done, 1)
            pe.wait_ge(ones_set, 1)
            pe.wait_ge(wabs, L)
            nc.tensor.matmul(acc[:, 0, 0:L], ones[:], wsum[:], start=True, stop=True).then_inc(wtot, 1)
            pe.wait_ge(id_in, 16)

            def group(g, q):
                for j in range(G):
                    i = G * g + j
                    pe.wait_ge(lo_ready[g], G * q + j + 1)
                    for n, part in enumerate((vlo, vhi)):
                        for k in range(KD):
                            c = (k * 2 + n) * P
                            last = nc.tensor.transpose(tp[:, i, c:c + P], part[:, i, k * P:(k + 1) * P], id16[:])
                    if j % 2:
                        last.then_inc(turned[g], 1)
                for j in range(2):
                    pe.wait_ge(vt_ready[g], 2 * q + j + 1)
                    if j == 0 and g == 0 and isinstance(q, int) and q == 0:
                        pe.wait_ge(wq, L)
                    for i in range(G * g + 2 * j, G * g + 2 * j + 2):
                        for n in range(2 * KD):
                            w = ta[:, bass.ds(q, 1), n // 2, :] if not isinstance(q, int) else ta[:, q:q + 1, n // 2, :]
                            last = nc.tensor.matmul(acc[:, i, :], vT[:, i, n * P:(n + 1) * P],
                                                    w.rearrange("p a d -> p (a d)"), start=n == 0, stop=n == 2 * KD - 1)
                last.then_inc(acc_ready[g], 1)

            pe.wait_ge(prep_read, len(fills))
            group(0, 0)
            with pe.Fori(1, L) as q:
                group(1, q - 1)
                group(0, q)
            group(1, L - 1)

            pe.wait_ge(q_in, 80)
            for i in range(NT):
                pe.wait_ge(norm_ready, i + 1)
                for k in range(KD):
                    c = (i % 2 * KD + k) * P
                    last = nc.tensor.transpose(bank(i // 2)[:, c:c + P], h0[:, i, k * P:(k + 1) * P], id32[:])
                if i % 2:
                    last.then_inc(qt_done, 1)
            for c in range(2):
                pe.wait_ge(qt_read, 2 * c + 2)
                for k in range(KD):
                    last = nc.tensor.matmul(bank(4 + c)[0:QC, :], wdq[:, k, :], qT[:, k, 512 * c:512 * (c + 1)],
                                            start=k == 0, stop=k == KD - 1)
                last.then_inc(qc_done, 1)
            pe.wait_ge(qt_read, 4)
            pe.wait_ge(fabs, 1)
            nc.tensor.matmul(bank(1)[:, 0:4], ones[:], fsum[:], start=True, stop=True).then_inc(ftot, 1)

            def rotary(b, n):
                if b + n > 0:
                    pe.wait_ge(a_read, 4 * b + n)
                for e in range(2):
                    m = 2 * n + e
                    last = nc.tensor.matmul(bank(0)[:, S * e:S * (e + 1)], wqr[:, 2 * R * m:2 * R * (m + 1)],
                                            qcT[:, S * b:S * (b + 1)], start=True, stop=True)
                last.then_inc(a_done, 1)

            def scores(i):
                b = i // 2
                tok = slice(P * i, P * (i + 1))
                pos = slice(P * (i % 2), P * (i % 2 + 1))
                pe.wait_ge(a_read, 4 * b + 4)
                if i >= 2:
                    pe.wait_ge(s_read, i - 1)
                for m in range(2):
                    dst = bank(2 + 2 * (i % 2) + m)
                    nc.tensor.matmul(dst, qcT[:, tok], ys[:, b, 8 * m:8 * m + 8, :].rearrange("q h k -> q (h k)"),
                                     start=True, stop=False)
                    nc.tensor.matmul(dst, bad[:, tok], negI[:], start=False, stop=False)
                    for r in range(4):
                        for n, t in enumerate((t1, t2)):
                            last = nc.tensor.matmul(dst[:, 2 * LK * r:2 * LK * (r + 1)], t[:, 4 * m + r, pos],
                                                    kbd[:, b, n, :], start=False, stop=n == 1 and r == 3)
                last.then_inc(s_done, 1)

            def turn_probs(i):
                pe.wait_ge(p_done, i + 1)
                if i >= 1:
                    pe.wait_ge(pt_read, i)
                for m in range(H // 2):
                    last = nc.tensor.transpose(bank(6 + m // 4)[:, m % 4 * P:(m % 4 + 1) * P],
                                               es[:, i % 2, 2 * m:2 * m + 2, :].rearrange("p h k -> p (h k)"), id32[:])
                last.then_inc(pt_done, 1)

            def values(i):
                pe.wait_ge(pt_read, i + 1)
                if i >= 1:
                    pe.wait_ge(x2_done, i)
                for m in range(H // 2):
                    last = nc.tensor.matmul(bank(1)[:, 0:D], pT[:, i % 2, P * m:P * (m + 1)], vn[:, i // 2, m, :],
                                            start=m == 0, stop=m == H // 2 - 1)
                last.then_inc(o_done, 1)

            pe.wait_ge(qc_read, 2)
            pe.wait_ge(kbd_ready, 1)
            pe.wait_ge(mask_ready, 1)
            for n in range(4):
                rotary(0, n)
            scores(0)
            scores(1)
            pe.wait_ge(fth_ready, 1)
            for b in range(B):
                for e in range(2):
                    if b + 1 < B:
                        rotary(b + 1, 2 * e)
                    turn_probs(2 * b + e)
                    if b + 1 < B:
                        rotary(b + 1, 2 * e + 1)
                    values(2 * b + e)
                if b + 1 < B:
                    scores(2 * b + 2)
                    scores(2 * b + 3)

            for i in range(NT):
                pe.wait_ge(ylo, i + 1)
                for n, part in enumerate((vhi, vlo)):
                    for k in range(KD):
                        c = (n * KD + k) * P
                        last = nc.tensor.transpose(tp[:, i, c:c + P], part[:, i, k * P:(k + 1) * P], id16[:])
                if i % 2:
                    last.then_inc(yt_done, 1)
            for n in range(NC * FJ):
                c, j = divmod(n, FJ)
                pe.wait_ge(yt_read, NT // 2)
                if n >= 2:
                    pe.wait_ge(hid_done, n - 1)
                for m in range(2):
                    for k in range(2 * KD):
                        last = nc.tensor.matmul(bank(2 * (n % 2) + m)[0:rows(j)],
                                                wf16[:, k // 2, F * m + P * j:F * m + P * j + rows(j)],
                                                yT[:, k % 2 * KD + k // 2, CH * c:CH * (c + 1)],
                                                start=k == 0, stop=k == 2 * KD - 1)
                last.then_inc(g_done, 1)
            for i in range(NT):
                c = i // (NT // NC)
                pe.wait_ge(hlo, FJ * (c + 1))
                t = slice(P * (i % (NT // NC)), P * (i % (NT // NC) + 1))
                for j in range(FJ):
                    r = slice(0, rows(j))
                    for n in range(2):
                        last = nc.tensor.matmul(tpf[:, i // 2, (i % 2) * D:(i % 2) * D + D], hid_hl[c][r, n, j, t],
                                                w316[r, j, :], start=j == 0 and n == 0, stop=j == FJ - 1 and n == 1)
                last.then_inc(f_done, 1)


def kernel(**inputs):
    import concourse.bacc as bacc
    import ml_dtypes
    from concourse.bass_utils import run_bass_kernel_spmd

    nc = bacc.Bacc("TRN2", target_bir_lowering=False, num_devices=1)
    a = {k: np.asarray(v) for k, v in inputs.items()}
    kr = a["L0_xattn_W_kr"]
    kr_swapped = np.concatenate([kr[:, R // 2:], kr[:, :R // 2]], axis=1)
    w3 = a["L0_ffn_w3"].T
    w3 = np.concatenate([w3, np.zeros((FJ * P - F, D), np.float32)]).reshape(FJ, P, D)
    freq = (1.0 / 10000.0 ** (np.arange(R // 2, dtype=np.float32) / (R // 2))).astype(np.float32)
    angle = np.arange(S, dtype=np.float32)[None, :] * freq[:, None]
    cos, sin = np.cos(angle), np.sin(angle)
    ck, sk = cos[:, :LK], sin[:, :LK]
    arrays = {
        "x": a["x"].reshape(T, D),
        "w_attn": a["L0_attn_W"].reshape(L, D, KD, P).transpose(3, 0, 2, 1).reshape(P, L, KD * D),
        "ident16": np.eye(P, dtype=np.float16),
        "ident32": np.eye(P, dtype=np.float32),
        "ctxT": a["ctx_2048"].reshape(B * LK, KD, P).transpose(2, 1, 0),
        "seg": a["itok_BxS_0_1023"].astype(np.int32).reshape(T),
        "w_kvc": a["L0_xattn_W_kvc"].reshape(KD, P, KVC).transpose(1, 0, 2),
        "w_dq": a["L0_xattn_W_dq"].reshape(KD, P, QC).transpose(1, 0, 2),
        "w_uqT": a["L0_xattn_W_uq"].reshape(QC, H, HD).transpose(2, 1, 0),
        "w_qr": a["L0_xattn_W_qr"],
        "w_uk": a["L0_xattn_W_uk"],
        "w_kr": np.stack([np.concatenate([kr, kr], axis=1), np.concatenate([kr_swapped, kr_swapped], axis=1)], axis=1),
        "w_uv": a["L0_xattn_W_uv"],
        "w_o": a["L0_xattn_W_o"].reshape(H, HD, D).transpose(1, 0, 2),
        "w12": np.concatenate([a["L0_ffn_w1"], a["L0_ffn_w2"]]).T.reshape(KD, P, 2 * F).transpose(1, 0, 2),
        "w3": w3.transpose(1, 0, 2),
        "rope_q": np.stack([np.tile(cos, (4, 1)), np.tile(sin, (4, 1))], axis=1),
        "rope_k": np.stack([np.tile(np.concatenate([u, v]), (2, 1)) for u, v in ((ck, ck), (-sk, sk), (ck, -ck), (sk, sk))],
                           axis=1),
        "key_index": np.arange(LK, dtype=np.float32)[:, None],
        "neg_eye": np.tile(NEG * np.eye(LK), (1, 8)).astype(ml_dtypes.bfloat16),
    }
    arrays = {k: np.ascontiguousarray(v) for k, v in arrays.items()}
    aps = {k: nc.dram_tensor(k, v.shape, mybir.dt.from_np(v.dtype), kind="ExternalInput").ap() for k, v in arrays.items()}
    out = nc.dram_tensor("out", (T, D), F32, kind="ExternalOutput").ap()
    build(nc, out=out, **aps)
    r = run_bass_kernel_spmd(nc, [arrays], core_ids=[0])
    return r.results[0]["out"].reshape(B, S, D)
```

```python
from contextlib import ExitStack

import numpy as np

import concourse.bass as bass
from concourse import mybir

F32 = mybir.dt.float32
F16 = mybir.dt.float16
BF16 = mybir.dt.bfloat16
I32 = mybir.dt.int32
U32 = mybir.dt.uint32
ALU = mybir.AluOpType
ACT = mybir.ActivationFunctionType
AX = mybir.AxisListType

P = 128
B, S, D = 4, 256, 256
T = B * S
NT = T // P
G = 2
GROUPS = NT // G
KD = D // P
L = 8
LK = 64
H, HD, R = 16, 128, 64
QC, KVC = 96, 64
LOOKBACK = 8
F = 704
FJ = (F + P - 1) // P
NEG = -1e30
LN_EPS = 1e-5
Q_EPS = 1e-5
MAGIC = 1.5 * 2.0**23


def build(nc, x, w_attn, ident16, ident32, ctxT, seg, w_kvc, w_dq, w_uqT, w_qr, w_ukv, w_kr, w_o, w12, w3, rope_q, rope_k,
          key_index, neg_eye, out):
    with ExitStack() as ctx:
        def sb(name, shape, dt):
            return ctx.enter_context(nc.sbuf_tensor(name, shape, dt))

        def ps(name, shape, dt):
            return ctx.enter_context(nc.psum_tensor(name, shape, dt))

        def sem(name):
            return ctx.enter_context(nc.semaphore(name))

        xs = sb("xs", [P, NT, D], F32)
        arena_a = sb("arena_a", [P, L * KD * D], F32)
        arena_o = sb("arena_o", [P, H * D], F32)
        arena_u = sb("arena_u", [P, 2 * H * HD], F32)
        wa = arena_a[:, :].rearrange("p (l c) -> p l c", l=L)
        t1 = arena_a[:, 0:H // 2 * S].rearrange("p (h s) -> p h s", h=H // 2)
        t2 = arena_a[:, H // 2 * S:H * S].rearrange("p (h s) -> p h s", h=H // 2)
        wo = arena_o[:, :].rearrange("p (h d) -> p h d", h=H)
        hid16 = arena_o[:, 0:FJ * 512].bitcast(F16).rearrange("p (n j t) -> p n j t", n=2, j=FJ)
        es = arena_u[:, 0:2 * H * LK].rearrange("p (n h k) -> p n h k", n=2, h=H)
        pT = arena_u[:, 2 * H * LK:4 * H * LK].rearrange("p (n c) -> p n c", n=2)
        arena_k = sb("arena_k", [P, KD * 2 * F + FJ * D], F32)
        wkvc = sb("wkvc", [P, KD, KVC], F32)
        wdq = sb("wdq", [P, KD, QC], F32)
        wqr = sb("wqr", [QC, H * R], F32)
        wkr = sb("wkr", [KVC, 2, 2 * R], F32)
        rq = sb("rq", [P, 2, S], F32)
        rk = sb("rk", [P, 4, LK], F32)
        kidx = sb("kidx", [LK, 1], F32)
        negI = sb("negI", [LK, 8 * LK], BF16)
        bad = sb("bad", [LK, T], BF16)
        id32 = sb("id32", [P, P], F32)
        kvc = sb("kvc", [KVC, B * LK], F32)
        kbd = sb("kbd", [P, B, 2, 2 * LK], F32)
        ys = sb("ys", [QC, B, H, LK], F32)
        vn = sb("vn", [P, B, H // 2, D], F32)
        qcT = sb("qcT", [QC, T], F32)
        smax = sb("smax", [P, 2, H], F32)
        ssum = sb("ssum", [P, 2, H], F32)
        srec = sb("srec", [P, 2, H], F32)
        fsum = sb("fsum", [P, 4], F32)
        fsc = sb("fsc", [P, 4], F32)
        fth = sb("fth", [P, 4], F32)
        fthn = sb("fthn", [P, 4], F32)
        ta = sb("ta", [P, L, KD, D], F16)
        tneg = sb("tneg", [P, KD * D], F16)
        id16 = sb("id16", [P, P], F16)
        ones = sb("ones", [P, P], F32)
        mtile = sb("mtile", [P, D], F32)
        wsum = sb("wsum", [P, L], F32)
        wscale = sb("wscale", [P, L], F32)
        wth = sb("wth", [P, L], F32)
        wthn = sb("wthn", [P, L], F32)
        stats = sb("stats", [P, NT, 6], F32)
        mv = sb("mv", [P, NT, 2], F32)
        rstd = sb("rstd", [P, NT], F32)
        rv = sb("rv", [P, NT], F32)
        rt = sb("rt", [P, NT], F32)
        h0 = sb("h0", [P, NT, D], F32)
        mx = sb("mx", [P, NT], F32)
        mh = sb("mh", [P, NT], F32)
        mxe = sb("mxe", [P, NT], F32)
        rc = sb("rc", [P, NT], F32)
        rr = sb("rr", [P, NT], F32)
        ss = sb("ss", [P, NT], F32)
        gg = sb("gg", [P, NT], F32)
        gm = sb("gm", [P, NT], F32)
        sg = sb("sg", [P, NT], F32)
        cs = sb("cs", [P, NT], F32)
        km = sb("km", [P, NT, D], F32)
        kk = sb("kk", [P, NT, D], F16)
        vhi = sb("vhi", [P, NT, D], F16)
        vlo = sb("vlo", [P, NT, D], F16)
        vT = sb("vT", [P, NT, 4 * P], F16)

        def part(arena, start, *dims):
            size = int(np.prod(dims))
            v = arena[:, start:start + size]
            if len(dims) == 2:
                v = v.rearrange("p (a b) -> p a b", a=dims[0])
            return v

        wukv = part(arena_k, 0, 4, HD)[0:KVC]
        wuqT = part(arena_k, 4 * HD, 2, QC)
        o_k = 4 * HD + 2 * QC
        knT = part(arena_k, o_k, 2, 2 * B * LK)
        rot = part(arena_k, o_k + 4 * B * LK, 4, B * LK)
        rawk = part(arena_k, o_k + 8 * B * LK, 2, B * LK)
        ctxs = part(arena_k, o_k + 10 * B * LK, KD, B * LK)
        wf = part(arena_k, 0, KD, 2 * F)
        w3s = part(arena_k, KD * 2 * F, FJ, D)
        taf = ta[:, :, :, :].rearrange("p l k d -> p (l k d)")
        wf16 = part(taf, 0, KD, 2 * F)
        kkf = kk[:, :, :].rearrange("p i d -> p (i d)")
        w316 = part(kkf, 0, FJ, D)
        fneg = vlo[:, :, :].rearrange("p i d -> p (i d)")
        vTf = vT[:, :, :].rearrange("p i c -> p (i c)")
        segs = vTf[0:LK, 0:2 * T].bitcast(I32)
        dist = km[:, :, :].rearrange("p i d -> p (i d)")[0:LK, 0:T]
        sgm = part(arena_u, 0, 2, 512)
        hid = part(arena_u, 1024, 2, 512)

        acc = ps("acc", [P, NT, D], F32)
        tp = ps("tp", [P, NT, 4 * P], F16)

        accf = acc[:, :, :].rearrange("p i d -> p (i d)").rearrange("p (b c) -> p b c", b=4)
        tpf = tp[:, :, :].rearrange("p i c -> p (i c)").bitcast(F32).rearrange("p (b c) -> p b c", b=4)

        def bank(n):
            return accf[:, n, :] if n < 4 else tpf[:, n - 4, :]

        x_in = sem("x_in")
        w_in = [sem(f"w_in{l}") for l in range(L)]
        id_in = sem("id_in")
        y_out = sem("y_out")
        k_in = sem("k_in")
        ukv_in = sem("ukv_in")
        uq_in = sem("uq_in")
        seg_in = sem("seg_in")
        wo_in = sem("wo_in")
        f_in = sem("f_in")
        mask_ready = sem("mask_ready")
        mask_part = sem("mask_part")
        q_in = sem("q_in")
        kvc_done = sem("kvc_done")
        kvc_read = sem("kvc_read")
        kn_done = sem("kn_done")
        kn_read = sem("kn_read")
        v_done = sem("v_done")
        v_read = sem("v_read")
        y_done = sem("y_done")
        y_read = sem("y_read")
        vn_done = sem("vn_done")
        vn_read_a = sem("vn_read_a")
        vn_read_v = sem("vn_read_v")
        dist_ready = sem("dist_ready")
        rot_in = sem("rot_in")
        kbd_ready = sem("kbd_ready")
        kbd_zero = sem("kbd_zero")
        std2 = sem("std2")
        var2 = sem("var2")
        norm_ready = sem("norm_ready")
        qt_done = sem("qt_done")
        qt_read = sem("qt_read")
        qc_done = sem("qc_done")
        qc_read = sem("qc_read")
        a_done = sem("a_done")
        a_read = sem("a_read")
        s_done = sem("s_done")
        s_read = sem("s_read")
        e_done = sem("e_done")
        r_done = sem("r_done")
        p_done = sem("p_done")
        pt_done = sem("pt_done")
        pt_read = sem("pt_read")
        o_done = sem("o_done")
        x2_done = sem("x2_done")
        fth_ready = sem("fth_ready")
        fabs = sem("fabs")
        ftot = sem("ftot")
        fq = sem("fq")
        norm3 = sem("norm3")
        yhi = sem("yhi")
        ylo = sem("ylo")
        yt_done = sem("yt_done")
        yt_read = sem("yt_read")
        g_done = sem("g_done")
        sig_done = sem("sig_done")
        hid_done = sem("hid_done")
        hhi = sem("hhi")
        hlo = sem("hlo")
        f_done = sem("f_done")
        ones_set = sem("ones_set")
        y_ready = sem("y_ready")
        wabs = sem("wabs")
        wtot = sem("wtot")
        wq = sem("wq")
        var_ready = sem("var_ready")
        std_ready = sem("std_ready")
        dv = sem("dv")
        r_ready = [sem(f"r_ready{g}") for g in range(GROUPS)]
        rounded = [sem(f"rounded{g}") for g in range(GROUPS)]
        k_ready = [sem(f"k_ready{g}") for g in range(GROUPS)]
        g_ready = [sem(f"g_ready{g}") for g in range(GROUPS)]
        hi_ready = [sem(f"hi_ready{g}") for g in range(GROUPS)]
        lo_ready = [sem(f"lo_ready{g}") for g in range(GROUPS)]
        turned = [sem(f"turned{g}") for g in range(GROUPS)]
        vt_ready = [sem(f"vt_ready{g}") for g in range(GROUPS)]
        acc_ready = [sem(f"acc_ready{g}") for g in range(GROUPS)]

        def before(q, g, d):
            return (q, g - d) if g >= d else (q - 1, g - d + GROUPS)

        half = lambda h: slice(LK * (h % 2), LK * (h % 2) + LK)
        qT = km[:, :, :].rearrange("p i d -> p (i d)").rearrange("p (k t) -> p k t", k=KD)
        yT = vT[:, :, :].rearrange("p i c -> p (i c)").rearrange("p (c t) -> p c t", c=2 * KD)
        hid_hl = [hid16, arena_a[:, 0:FJ * 512].bitcast(F16).rearrange("p (n j t) -> p n j t", n=2, j=FJ)]
        SCALE = 1.0 / float(np.sqrt(np.float32(HD + R)))
        CH = 512
        NC = T // CH
        rows = lambda j: min(P, F - j * P)

        def value_copies(engine, copy, m, hp, read):
            for e in range(2):
                engine.wait_ge(vn_done, 2 * hp + e + 1)
                copy(vn[half(e), :, bass.ds(hp, 1), :].rearrange("p (n m) h d -> p m n (h d)", m=2)[:, m],
                     bank(7 - e)[half(m), :].rearrange("p (n d) -> p n d", n=2)).then_inc(read, 1)

        block = ctx.enter_context(nc.Block())

        @block.sync
        def _(sp):
            sp.dma_start(xs[:], x.rearrange("(i p) d -> p i d", p=P)).then_inc(x_in, 16)
            sp.dma_start(wukv, w_ukv[0]).then_inc(ukv_in, 16)
            sp.dma_start(wuqT, w_uqT[0]).then_inc(uq_in, 16)
            for l in range(L):
                sp.dma_start(wa[:, l, :], w_attn[:, l, :]).then_inc(w_in[l], 16)
            sp.dma_start(wo, w_o).then_inc(wo_in, 16)
            with sp.Fori(1, H // 2) as q:
                sp.wait_ge(v_done, q)
                sp.dma_start(wukv, w_ukv[bass.ds(q, 1)].rearrange("a p n c -> p (a n) c")).then_inc(ukv_in, 16)
                sp.wait_ge(y_done, q)
                sp.dma_start(wuqT, w_uqT[bass.ds(q, 1)].rearrange("a p n c -> p (a n) c")).then_inc(uq_in, 16)
            sp.wait_ge(vn_done, H)
            sp.wait_ge(kbd_ready, 1)
            sp.dma_start(wf, w12).then_inc(f_in, 16)
            sp.dma_start(w3s[:, 0:FJ - 1, :], w3[:, 0:FJ - 1, :]).then_inc(f_in, 16)
            sp.dma_start(w3s[0:F - (FJ - 1) * P, FJ - 1, :], w3[0:F - (FJ - 1) * P, FJ - 1, :]).then_inc(f_in, 16)
            for i in range(NT):
                sp.wait_ge(y_ready, i + 1)
                sp.dma_start(out[P * i:P * (i + 1), :], xs[:, i, :]).then_inc(y_out, 16)
            sp.wait_ge(y_out, 16 * NT)

        @block.scalar
        def _(act):
            act.dma_start(ctxs, ctxT).then_inc(k_in, 16)
            act.dma_start(wkvc[:], w_kvc).then_inc(k_in, 16)
            act.dma_start(wkr[:], w_kr).then_inc(k_in, 16)
            act.dma_start(rk[:], rope_k).then_inc(k_in, 16)
            act.dma_start(segs, seg.partition_broadcast(LK)).then_inc(seg_in, 16)
            act.dma_start(kidx[:], key_index).then_inc(seg_in, 16)
            act.dma_start(id16[:], ident16).then_inc(id_in, 16)
            act.wait_ge(var_ready, 1)
            nc.scalar.activation(rt[:], rv[:], ACT.Sqrt).then_inc(std_ready, 1)
            act.wait_ge(seg_in, 32)
            nc.scalar.activation(dist, segs, ACT.Abs, bias=kidx[:]).then_inc(dist_ready, 1)
            act.wait_ge(kvc_done, 1)
            nc.scalar.copy(kvc[:], bank(6)[0:KVC, 0:B * LK]).then_inc(kvc_read, 1)
            act.wait_ge(kvc_done, 2)
            nc.scalar.copy(rawk.rearrange("p n c -> p (n c)"), bank(7)).then_inc(kvc_read, 1)
            act.dma_start(wdq[:], w_dq).then_inc(q_in, 16)
            act.dma_start(wqr[:], w_qr).then_inc(q_in, 16)
            act.dma_start(rq[:], rope_q).then_inc(q_in, 16)
            act.dma_start(id32[:], ident32).then_inc(q_in, 16)
            act.dma_start(negI[:], neg_eye).then_inc(q_in, 16)
            act.wait_ge(ones_set, 2)

            def round_group(q, g):
                act.wait_ge(r_ready[g], q + 1)
                for i in range(G * g, G * g + G):
                    src = h0 if isinstance(q, int) and q == 0 else acc
                    nc.scalar.activation(km[:, i, :], src[:, i, :], ACT.Identity, scale=rr[:, i:i + 1],
                                         bias=mtile[:, 0:1]).then_inc(rounded[g], 1)

            def high_group(q, g):
                act.wait_ge(g_ready[g], q + 1)
                for j in range(G):
                    i = G * g + j
                    act.wait_ge(k_ready[g], G * q + j + 1)
                    nc.scalar.activation(vhi[:, i, :], kk[:, i, :], ACT.Copy, scale=gm[:, i:i + 1]).then_inc(hi_ready[g], 1)

            def copy_group(q, g):
                act.wait_ge(turned[g], q + 1)
                nc.scalar.copy(vT[:, G * g:G * g + G, :].bitcast(U32),
                               tp[:, G * (g % 2):G * (g % 2) + G, :].bitcast(U32)).then_inc(vt_ready[g], 1)

            def key_copies(q, g):
                if g == 1:
                    act.wait_ge(kn_done, q + 1)
                    nc.scalar.copy(knT[:, 0, :], bank(6)).then_inc(kn_read, 1)
                elif g == 3:
                    act.wait_ge(y_done, q + 1)
                    nc.scalar.copy(ys[:, :, bass.ds(2 * q, 2), :].rearrange("q b e k -> q e b k"),
                                   bank(6)[0:QC, :].rearrange("q (e b k) -> q e b k", e=2, b=B)).then_inc(y_read, 1)
                elif g == 0:
                    value_copies(act, nc.scalar.copy, 0, q - 1, vn_read_a)

            for g in range(GROUPS):
                if g > 0:
                    high_group(*before(0, g, 1))
                round_group(0, g)
                if g > 0:
                    copy_group(*before(0, g, 1))
                    key_copies(0, g)
            with act.Fori(1, L) as q:
                for g in range(GROUPS):
                    high_group(*before(q, g, 1))
                    round_group(q, g)
                    copy_group(*before(q, g, 1))
                    key_copies(q, g)
            high_group(L - 1, GROUPS - 1)
            copy_group(L - 1, GROUPS - 1)
            key_copies(L, 0)

            act.wait_ge(var2, 1)
            nc.scalar.activation(rt[:], rv[:], ACT.Sqrt).then_inc(std2, 1)
            for j in range(NT // 2):
                act.wait_ge(qt_done, j + 1)
                nc.scalar.copy(qT[:, :, 2 * P * j:2 * P * (j + 1)].rearrange("p k (i t) -> p i k t", i=2),
                               bank(j).rearrange("p (i k t) -> p i k t", i=2, k=KD)).then_inc(qt_read, 1)
            for c in range(2):
                act.wait_ge(qc_done, c + 1)
                nc.scalar.copy(qcT[:, 512 * c:512 * (c + 1)], bank(4 + c)[0:QC, :]).then_inc(qc_read, 1)

            def exps(i):
                act.wait_ge(s_read, i + 1)
                nc.scalar.activation(es[:, i % 2], es[:, i % 2], ACT.Exp, scale=SCALE).then_inc(e_done, 1)

            def copy_probs(i):
                act.wait_ge(pt_done, i + 1)
                nc.scalar.copy(pT[:, i % 2, :], tpf[:, 2:4, :].rearrange("p b c -> p (b c)")).then_inc(pt_read, 1)

            exps(0)
            exps(1)
            for b in range(B):
                copy_probs(2 * b)
                copy_probs(2 * b + 1)
                if b + 1 < B:
                    exps(2 * b + 2)
                    exps(2 * b + 3)
            act.wait_ge(var2, 2)
            nc.scalar.activation(rt[:], rv[:], ACT.Sqrt).then_inc(std2, 1)
            for i in range(NT):
                act.wait_ge(norm3, i + 1)
                nc.scalar.copy(vhi[:, i, :], h0[:, i, :]).then_inc(yhi, 1)
            for j in range(NT // 2):
                act.wait_ge(yt_done, j + 1)
                nc.scalar.copy(yT[:, :, 2 * P * j:2 * P * (j + 1)].bitcast(U32).rearrange("p c (i t) -> p i c t", i=2),
                               tp[:, 2 * j:2 * j + 2, :].bitcast(U32).rearrange("p i (c t) -> p i c t", c=2 * KD)
                               ).then_inc(yt_read, 1)
            for n in range(NC * FJ):
                c, j = divmod(n, FJ)
                r = slice(0, rows(j))
                act.wait_ge(g_done, n + 1)
                if n >= 2:
                    act.wait_ge(hid_done, n - 1)
                nc.scalar.activation(sgm[r, n % 2, :], bank(2 * (n % 2))[r], ACT.Sigmoid, scale=1.0 / 2048).then_inc(sig_done, 1)
                act.wait_ge(hid_done, n + 1)
                nc.scalar.copy(hid_hl[c][r, 0, j, :], hid[r, n % 2, :]).then_inc(hhi, 1)

        @block.gpsimd
        def _(pool):
            nc.gpsimd.memset(ones[:], 1.0).then_inc(ones_set, 1)
            nc.gpsimd.memset(mtile[:], MAGIC).then_inc(ones_set, 1)

            pool.wait_ge(ones_set, 2)

            nc.gpsimd.memset(kbd[:], 0.0).then_inc(kbd_zero, 1)
            pool.wait_ge(k_in, 64)
            pool.wait_ge(kvc_read, 2)
            for n, (src, dst) in enumerate(((0, 0), (1, 1), (1, 2), (0, 3))):
                last = nc.gpsimd.tensor_tensor(rot[:, dst, :].rearrange("p (b k) -> p b k", b=B),
                                               rawk[:, src, :].rearrange("p (b k) -> p b k", b=B),
                                               rk[:, dst:dst + 1, :].to_broadcast([P, B, LK]), ALU.mult)
            last.then_inc(rot_in, 1)
            pool.wait_ge(rot_in, 1)
            pool.wait_ge(kbd_zero, 1)
            for n in range(2):
                for e in range(2):
                    last = nc.gpsimd.tensor_tensor(kbd[half(e), :, n, half(e)],
                                                   rot[half(e), 2 * n, :].rearrange("p (b k) -> p b k", b=B),
                                                   rot[half(e), 2 * n + 1, :].rearrange("p (b k) -> p b k", b=B), ALU.add)
            last.then_inc(kbd_ready, 1)
            pool.wait_ge(kbd_ready, 1)

            def integers(q, g):
                for j in range(G):
                    i = G * g + j
                    pool.wait_ge(rounded[g], G * q + j + 1)
                    nc.gpsimd.tensor_tensor(kk[:, i, :], km[:, i, :], mtile[:], ALU.subtract).then_inc(k_ready[g], 1)

            for g in range(GROUPS):
                integers(0, g)
            with pool.Fori(1, L) as q:
                for g in range(GROUPS):
                    integers(q, g)
            for i in range(NT):
                pool.wait_ge(r_done, i + 1)
                nc.gpsimd.tensor_tensor(es[:, i % 2], es[:, i % 2], srec[:, i % 2, :].unsqueeze(2).to_broadcast([P, H, LK]),
                                        ALU.mult).then_inc(p_done, 1)

        @block.vector
        def _(dve):
            done = [0]

            def link(ins):
                done[0] += 1
                ins.then_inc(dv, 1)
                dve.wait_ge(dv, done[0])

            dve.wait_ge(x_in, 16)
            for i in range(NT):
                last = nc.vector.bn_stats(stats[:, i, :], xs[:, i, :])
            link(last)
            for i in range(NT):
                last = nc.vector.bn_aggr(mv[:, i, :], stats[:, i, :])
            link(last)
            nc.vector.tensor_scalar(rv[:], mv[:, :, 1], LN_EPS, None, ALU.add).then_inc(var_ready, 1)
            dve.wait_ge(dist_ready, 1)
            nc.vector.tensor_scalar(bad[:], dist, float(LOOKBACK) / 2, None, ALU.is_gt).then_inc(mask_ready, 1)
            for l in range(L):
                dve.wait_ge(w_in[l], 16)
                nc.vector.tensor_reduce(wsum[:, l:l + 1], wa[:, l, :], axis=AX.X, op=ALU.add,
                                        apply_absolute_value=True).then_inc(wabs, 1)
            dve.wait_ge(std_ready, 1)
            dve.wait_ge(var_ready, 1)
            link(nc.vector.reciprocal(rstd[:], rt[:]))
            link(nc.vector.tensor_tensor(rt[:], rstd[:], rstd[:], ALU.mult))
            link(nc.vector.tensor_tensor(rt[:], rt[:], rv[:], ALU.mult))
            link(nc.vector.tensor_scalar(rt[:], rt[:], -0.5, 1.5, ALU.mult, ALU.add))
            link(nc.vector.tensor_tensor(rstd[:], rstd[:], rt[:], ALU.mult))
            for i in range(NT):
                last = nc.vector.tensor_scalar(h0[:, i, :], xs[:, i, :], mv[:, i, 0:1], rstd[:, i:i + 1],
                                               ALU.subtract, ALU.mult)
            link(last)
            link(nc.vector.tensor_reduce(mx[:], h0[:], axis=AX.X, op=ALU.max, apply_absolute_value=True))
            dve.wait_ge(wtot, 1)
            link(nc.vector.tensor_scalar(wscale[:], acc[:, 0, 0:L], 1.0 / (D * D), Q_EPS, ALU.mult, ALU.add))
            nc.vector.tensor_scalar(wth[:], wscale[:], 0.5, None, ALU.mult)
            link(nc.vector.tensor_scalar(wthn[:], wscale[:], -0.5, None, ALU.mult))
            link(nc.vector.tensor_scalar(mxe[:], mx[:], Q_EPS, None, ALU.add))
            link(nc.vector.reciprocal(rc[:], mxe[:]))
            for g in range(GROUPS):
                s = slice(G * g, G * g + G)
                nc.vector.tensor_scalar(rr[:, s], rc[:, s], 127.0, None, ALU.mult).then_inc(r_ready[g], 1)
            for g in range(GROUPS):
                dve.wait_ge(r_ready[g], 1)
            link(nc.vector.reciprocal(gg[:], rr[:]))
            for g in range(GROUPS):
                s = slice(G * g, G * g + G)
                nc.vector.tensor_scalar(gm[:, s].bitcast(I32), gg[:, s].bitcast(I32), 0x7FFFFF, 0x43000000,
                                        ALU.bitwise_and, ALU.bitwise_or).then_inc(g_ready[g], 1)
            link(nc.vector.tensor_scalar(sg[:].bitcast(I32), gg[:].bitcast(I32), 0x7F800000, None, ALU.bitwise_and))
            link(nc.vector.tensor_scalar(cs[:], sg[:], 1.0 / 128.0, wscale[:, 0:1], ALU.mult, ALU.mult))

            def ternary_layer(l):
                if l > 0:
                    dve.wait_ge(wq, l)
                link(nc.vector.tensor_scalar(tneg[:], wa[:, l, :], wthn[:, l:l + 1], None, ALU.is_lt))
                nc.vector.scalar_tensor_tensor(ta[:, l].rearrange("p k d -> p (k d)"), wa[:, l, :], wth[:, l:l + 1],
                                               tneg[:], ALU.is_gt, ALU.subtract).then_inc(wq, 1)

            def low_tile(q, g, j):
                i = G * g + j
                dve.wait_ge(hi_ready[g], G * q + j + 1)
                nc.vector.scalar_tensor_tensor(vlo[:, i, :], kk[:, i, :], gm[:, i:i + 1], vhi[:, i, :],
                                               ALU.mult, ALU.subtract).then_inc(lo_ready[g], 1)

            def key_copies(q, g):
                if g == 2:
                    dve.wait_ge(v_done, q + 1)
                    nc.vector.tensor_copy(knT[:, 1, :], bank(7)).then_inc(v_read, 1)
                elif g == 0:
                    value_copies(dve, nc.vector.tensor_copy, 1, q - 1, vn_read_v)

            for l in range(2):
                ternary_layer(l)
            for g in range(GROUPS):
                if g > 0:
                    for j in range(G):
                        low_tile(*before(0, g, 1), j)
                if g + 1 < GROUPS:
                    ternary_layer(2 * g + 2)
                    ternary_layer(2 * g + 3)
                key_copies(0, g) if g else None
            base = done[0]
            STEPS = 8

            def scales(q, g):
                s = slice(G * g, G * g + G)
                start = base + STEPS * (GROUPS * (q - 1) + g)
                at = [0]

                def step(ins):
                    at[0] += 1
                    ins.then_inc(dv, 1)

                def stepped():
                    dve.wait_ge(dv, start + at[0])

                earlier = before(q, g, 1)
                dve.wait_ge(acc_ready[g], q)
                step(nc.vector.tensor_reduce(mx[:, s], acc[:, s, :], axis=AX.X, op=ALU.max, apply_absolute_value=True))
                stepped()
                step(nc.vector.tensor_tensor(mh[:, s], mx[:, s], cs[:, s], ALU.mult))
                stepped()
                step(nc.vector.tensor_scalar(mxe[:, s], mh[:, s], Q_EPS, None, ALU.add))
                stepped()
                step(nc.vector.reciprocal(rc[:, s], mxe[:, s]))
                stepped()
                nc.vector.scalar_tensor_tensor(rr[:, s], rc[:, s], 127.0, cs[:, s], ALU.mult, ALU.mult).then_inc(r_ready[g], 1)
                step(nc.vector.tensor_scalar(ss[:, s], rc[:, s], 127.0, None, ALU.mult))
                low_tile(*earlier, 0)
                stepped()
                step(nc.vector.reciprocal(gg[:, s], ss[:, s]))
                low_tile(*earlier, 1)
                stepped()
                nc.vector.tensor_scalar(gm[:, s].bitcast(I32), gg[:, s].bitcast(I32), 0x7FFFFF, 0x43000000,
                                        ALU.bitwise_and, ALU.bitwise_or).then_inc(g_ready[g], 1)
                step(nc.vector.tensor_scalar(sg[:, s].bitcast(I32), gg[:, s].bitcast(I32), 0x7F800000, None,
                                             ALU.bitwise_and))
                key_copies(q, g)
                stepped()
                step(nc.vector.tensor_scalar(cs[:, s], sg[:, s], 1.0 / 128.0, wscale[:, bass.ds(q, 1)], ALU.mult,
                                             ALU.mult))
                stepped()

            with dve.Fori(1, L) as q:
                for g in range(GROUPS):
                    scales(q, g)
            for j in range(G):
                low_tile(L - 1, GROUPS - 1, j)
            value_copies(dve, nc.vector.tensor_copy, 1, H // 2 - 1, vn_read_v)
            done[0] = base + STEPS * GROUPS * (L - 1)

            def norm_scales(n, times):
                for i in range(NT):
                    last = nc.vector.bn_stats(stats[:, i, :], xs[:, i, :])
                link(last)
                for i in range(NT):
                    last = nc.vector.bn_aggr(mv[:, i, :], stats[:, i, :])
                link(last)
                nc.vector.tensor_scalar(rv[:], mv[:, :, 1], LN_EPS, None, ALU.add).then_inc(var2, 1)
                dve.wait_ge(std2, n)
                dve.wait_ge(var2, n)
                link(nc.vector.reciprocal(rstd[:], rt[:]))
                link(nc.vector.tensor_tensor(rt[:], rstd[:], rstd[:], ALU.mult))
                link(nc.vector.tensor_tensor(rt[:], rt[:], rv[:], ALU.mult))
                link(nc.vector.tensor_scalar(rt[:], rt[:], -0.5 * times, 1.5 * times, ALU.mult, ALU.add))
                link(nc.vector.tensor_tensor(rstd[:], rstd[:], rt[:], ALU.mult))

            for g in range(GROUPS):
                dve.wait_ge(acc_ready[g], L)
                for i in range(G * g, G * g + G):
                    last = nc.vector.scalar_tensor_tensor(xs[:, i, :], acc[:, i, :], cs[:, i:i + 1], xs[:, i, :],
                                                          ALU.mult, ALU.add)
            link(last)
            norm_scales(1, 1.0)
            for i in range(NT):
                nc.vector.tensor_scalar(h0[:, i, :], xs[:, i, :], mv[:, i, 0:1], rstd[:, i:i + 1],
                                        ALU.subtract, ALU.mult).then_inc(norm_ready, 1)
            dve.wait_ge(f_in, 48)
            link(nc.vector.memset(fsum[:], 0.0))
            for n in range(2):
                nc.vector.tensor_reduce(fsum[:, n:n + 1], wf[:, :, F * n:F * n + F], axis=AX.XY, op=ALU.add,
                                        apply_absolute_value=True)
            nc.vector.tensor_reduce(fsum[:, 2:3], w3s[:, 0:FJ - 1, :], axis=AX.XY, op=ALU.add, apply_absolute_value=True)
            nc.vector.tensor_reduce(fsum[0:rows(FJ - 1), 3:4], w3s[0:rows(FJ - 1), FJ - 1, :], axis=AX.X, op=ALU.add,
                                    apply_absolute_value=True).then_inc(fabs, 1)

            def turn(b):
                for n in range(4):
                    turn_fill(b, n)

            def turn_fill(b, n):
                dve.wait_ge(a_done, 4 * b + n + 1)
                if b > 0 and n == 0:
                    dve.wait_ge(s_done, 2 * b)
                src = bank(0).rearrange("p (h s) -> p h s", h=2)
                nc.vector.tensor_tensor(t1[:, 2 * n:2 * n + 2, :], src, rq[:, 0:1, :].to_broadcast([P, 2, S]), ALU.mult)
                nc.vector.tensor_tensor(t2[:, 2 * n:2 * n + 2, :], src, rq[:, 1:2, :].to_broadcast([P, 2, S]),
                                        ALU.mult).then_inc(a_read, 1)

            def less_max(i):
                src = (accf[:, 2:4, :] if i % 2 == 0 else tpf[:, 0:2, :]).rearrange("p b (h k) -> p (b h) k", k=LK)
                dve.wait_ge(s_done, i + 1)
                if i >= 2:
                    dve.wait_ge(pt_done, i - 1)
                link(nc.vector.tensor_reduce(smax[:, i % 2, :], src, axis=AX.X, op=ALU.max))
                nc.vector.tensor_tensor(es[:, i % 2], src, smax[:, i % 2, :].unsqueeze(2).to_broadcast([P, H, LK]),
                                        ALU.subtract).then_inc(s_read, 1)

            def sums(i):
                dve.wait_ge(e_done, i + 1)
                link(nc.vector.tensor_reduce(ssum[:, i % 2, :], es[:, i % 2], axis=AX.X, op=ALU.add))
                nc.vector.reciprocal(srec[:, i % 2, :], ssum[:, i % 2, :]).then_inc(r_done, 1)

            def add_attn(i):
                dve.wait_ge(o_done, i + 1)
                nc.vector.tensor_tensor(xs[:, i, :], bank(1)[:, 0:D], xs[:, i, :], ALU.add).then_inc(x2_done, 1)

            dve.wait_ge(q_in, 80)
            turn(0)
            for i in range(2):
                less_max(i)
            for i in range(2):
                sums(i)
            dve.wait_ge(ftot, 1)
            link(nc.vector.tensor_scalar(fsc[:, 0:2], bank(1)[:, 0:2], 1.0 / (F * D), 1e-8, ALU.mult, ALU.add))
            link(nc.vector.tensor_reduce(fsum[:, 0:1], bank(1)[:, 2:4], axis=AX.X, op=ALU.add))
            link(nc.vector.tensor_scalar(fsc[:, 2:3], fsum[:, 0:1], 1.0 / (F * D), 1e-8, ALU.mult, ALU.add))
            nc.vector.tensor_scalar(fth[:, 0:3], fsc[:, 0:3], 0.5, None, ALU.mult)
            nc.vector.tensor_scalar(fthn[:, 0:3], fsc[:, 0:3], -0.5, None, ALU.mult).then_inc(fth_ready, 1)
            dve.wait_ge(fth_ready, 1)

            def ternary(n):
                if n < 2 * KD:
                    k, m = divmod(n, 2)
                    w, o, th = wf[:, k, F * m:F * m + F], wf16[:, k, F * m:F * m + F], m
                    tmp = fneg[:, 0:F]
                elif n == 2 * KD:
                    w, o, th = w3s[:, 0:FJ - 1, :], w316[:, 0:FJ - 1, :], 2
                    tmp = fneg[:, 0:(FJ - 1) * D].rearrange("p (j d) -> p j d", j=FJ - 1)
                else:
                    r = slice(0, rows(FJ - 1))
                    w, o, th = w3s[r, FJ - 1, :], w316[r, FJ - 1, :], 2
                    tmp = fneg[r, 0:D]
                q = slice(0, w.shape[0])
                link(nc.vector.tensor_scalar(tmp, w, fthn[q, th:th + 1], None, ALU.is_lt))
                link(nc.vector.scalar_tensor_tensor(o, w, fth[q, th:th + 1], tmp, ALU.is_gt, ALU.subtract))

            for b in range(B):
                for e in range(2):
                    if b + 1 < B:
                        turn_fill(b + 1, 2 * e)
                        turn_fill(b + 1, 2 * e + 1)
                    add_attn(2 * b + e)
                if b < 3:
                    ternary(2 * b)
                    ternary(2 * b + 1)
                if b + 1 < B:
                    for i in (2 * b + 2, 2 * b + 3):
                        less_max(i)
                    for i in (2 * b + 2, 2 * b + 3):
                        sums(i)
            dve.wait_ge(x2_done, NT)
            norm_scales(2, 2048.0)
            for i in range(NT):
                nc.vector.tensor_scalar(h0[:, i, :], xs[:, i, :], mv[:, i, 0:1], rstd[:, i:i + 1],
                                        ALU.subtract, ALU.mult).then_inc(norm3, 1)
            for i in range(NT):
                dve.wait_ge(yhi, i + 1)
                nc.vector.tensor_tensor(vlo[:, i, :], h0[:, i, :], vhi[:, i, :], ALU.subtract).then_inc(ylo, 1)

            def low(n):
                c, j = divmod(n, FJ)
                r = slice(0, rows(j))
                dve.wait_ge(hhi, n + 1)
                nc.vector.tensor_tensor(hid_hl[c][r, 1, j, :], hid[r, n % 2, :], hid_hl[c][r, 0, j, :],
                                        ALU.subtract).then_inc(hlo, 1)

            for n in range(NC * FJ):
                c, j = divmod(n, FJ)
                r = slice(0, rows(j))
                dve.wait_ge(sig_done, n + 1)
                if n >= 2:
                    dve.wait_ge(hlo, n - 1)
                nc.vector.scalar_tensor_tensor(hid[r, n % 2, :], bank(2 * (n % 2) + 1)[r], 1.0 / 16, sgm[r, n % 2, :],
                                               ALU.mult, ALU.mult).then_inc(hid_done, 1)
                if n >= 1:
                    low(n - 1)
            low(NC * FJ - 1)
            for i in range(NT):
                if i % 2 == 0:
                    dve.wait_ge(f_done, i + 2)
                nc.vector.scalar_tensor_tensor(xs[:, i, :], tpf[:, i // 2, (i % 2) * D:(i % 2) * D + D], 1.0 / 128,
                                               xs[:, i, :], ALU.mult, ALU.add).then_inc(y_ready, 1)

        @block.tensor
        def _(pe):
            pe.wait_ge(k_in, 64)
            for k in range(KD):
                last = nc.tensor.matmul(bank(6)[0:KVC, 0:B * LK], wkvc[:, k, :], ctxs[:, k, :], start=k == 0, stop=k == KD - 1)
            last.then_inc(kvc_done, 1)
            pe.wait_ge(kvc_read, 1)
            for m in range(2):
                last = nc.tensor.matmul(bank(7)[:, B * LK * m:B * LK * (m + 1)], wkr[:, m, :], kvc[:], start=True, stop=True)
            last.then_inc(kvc_done, 1)
            pe.wait_ge(ones_set, 1)
            pe.wait_ge(wabs, L)
            nc.tensor.matmul(acc[:, 0, 0:L], ones[:], wsum[:], start=True, stop=True).then_inc(wtot, 1)
            pe.wait_ge(id_in, 16)

            def turn_group(q, g, first=False):
                if not first:
                    pe.wait_ge(vt_ready[(g - 2) % GROUPS], q + 1 if g >= 2 else q)
                for j in range(G):
                    i = G * g + j
                    pe.wait_ge(lo_ready[g], G * q + j + 1)
                    for n, half_of in enumerate((vlo, vhi)):
                        for k in range(KD):
                            c = (k * 2 + n) * P
                            last = nc.tensor.transpose(tp[:, G * (g % 2) + j, c:c + P], half_of[:, i, k * P:(k + 1) * P],
                                                       id16[:])
                last.then_inc(turned[g], 1)

            def multiply_group(q, g):
                pe.wait_ge(vt_ready[g], q + 1)
                if g == 0:
                    pe.wait_ge(wq, q + 1)
                for i in range(G * g, G * g + G):
                    for n in range(2 * KD):
                        w = ta[:, bass.ds(q, 1), n // 2, :].rearrange("p a d -> p (a d)")
                        last = nc.tensor.matmul(acc[:, i, :], vT[:, i, n * P:(n + 1) * P], w, start=n == 0,
                                                stop=n == 2 * KD - 1)
                last.then_inc(acc_ready[g], 1)

            def key_products(q, g, first=False):
                bkt = B * LK
                if g == 0:
                    pe.wait_ge(ukv_in, 16 * q + 16)
                    if not first:
                        pe.wait_ge(vn_read_a, 2 * q)
                        pe.wait_ge(vn_read_v, 2 * q)
                    for e in range(2):
                        last = nc.tensor.matmul(bank(6)[:, bkt * e:bkt * (e + 1)], wukv[:, e, :], kvc[:],
                                                start=True, stop=True)
                    last.then_inc(kn_done, 1)
                elif g == 1:
                    if first:
                        pe.wait_ge(kvc_read, 2)
                    for e in range(2):
                        last = nc.tensor.matmul(bank(7)[:, bkt * e:bkt * (e + 1)], wukv[:, 2 + e, :], kvc[:],
                                                start=True, stop=True)
                    last.then_inc(v_done, 1)
                elif g == 2:
                    pe.wait_ge(kn_read, q + 1)
                    pe.wait_ge(uq_in, 16 * q + 16)
                    for e in range(2):
                        last = nc.tensor.matmul(bank(6)[0:QC, bkt * e:bkt * (e + 1)], wuqT[:, e, :], knT[:, 0, bkt * e:bkt * (e + 1)],
                                                start=True, stop=True)
                    last.then_inc(y_done, 1)
                else:
                    if first:
                        pe.wait_ge(wo_in, 16)
                    for e in range(2):
                        pe.wait_ge(*((v_read, q + 1) if e == 0 else (y_read, q + 1)))
                        for m in range(2):
                            o = bkt * e + 2 * LK * m
                            w = wo[:, bass.ds(2 * q + e, 1), :].rearrange("p a d -> p (a d)")
                            last = nc.tensor.matmul(bank(7 - e)[:, D * m:D * (m + 1)], knT[:, 1, o:o + 2 * LK], w,
                                                    start=True, stop=True)
                        last.then_inc(vn_done, 1)

            for g in range(GROUPS):
                if g >= 2:
                    multiply_group(*before(0, g, 2))
                if g >= 1:
                    turn_group(*before(0, g, 1), first=g < 3)
                key_products(0, g, first=True)
            with pe.Fori(1, L) as q:
                for g in range(GROUPS):
                    multiply_group(*before(q, g, 2))
                    turn_group(*before(q, g, 1))
                    key_products(q, g)
            multiply_group(L - 1, GROUPS - 2)
            turn_group(L - 1, GROUPS - 1)
            multiply_group(L - 1, GROUPS - 1)

            pe.wait_ge(q_in, 80)
            for i in range(NT):
                pe.wait_ge(norm_ready, i + 1)
                for k in range(KD):
                    c = (i % 2 * KD + k) * P
                    last = nc.tensor.transpose(bank(i // 2)[:, c:c + P], h0[:, i, k * P:(k + 1) * P], id32[:])
                if i % 2:
                    last.then_inc(qt_done, 1)
            for c in range(2):
                pe.wait_ge(qt_read, 2 * c + 2)
                for k in range(KD):
                    last = nc.tensor.matmul(bank(4 + c)[0:QC, :], wdq[:, k, :], qT[:, k, 512 * c:512 * (c + 1)],
                                            start=k == 0, stop=k == KD - 1)
                last.then_inc(qc_done, 1)
            pe.wait_ge(qt_read, 4)
            pe.wait_ge(vn_read_a, H)
            pe.wait_ge(vn_read_v, H)
            pe.wait_ge(fabs, 1)
            nc.tensor.matmul(bank(1)[:, 0:4], ones[:], fsum[:], start=True, stop=True).then_inc(ftot, 1)

            def rotary(b, n):
                if b + n > 0:
                    pe.wait_ge(a_read, 4 * b + n)
                for e in range(2):
                    m = 2 * n + e
                    last = nc.tensor.matmul(bank(0)[:, S * e:S * (e + 1)], wqr[:, 2 * R * m:2 * R * (m + 1)],
                                            qcT[:, S * b:S * (b + 1)], start=True, stop=True)
                last.then_inc(a_done, 1)

            def scores(i):
                b = i // 2
                tok = slice(P * i, P * (i + 1))
                pos = slice(P * (i % 2), P * (i % 2 + 1))
                pe.wait_ge(a_read, 4 * b + 4)
                if i >= 2:
                    pe.wait_ge(s_read, i - 1)
                for m in range(2):
                    dst = bank(2 + 2 * (i % 2) + m)
                    nc.tensor.matmul(dst, qcT[:, tok], ys[:, b, 8 * m:8 * m + 8, :].rearrange("q h k -> q (h k)"),
                                     start=True, stop=False)
                    nc.tensor.matmul(dst, bad[:, tok], negI[:], start=False, stop=False)
                    for r in range(4):
                        for n, t in enumerate((t1, t2)):
                            last = nc.tensor.matmul(dst[:, 2 * LK * r:2 * LK * (r + 1)], t[:, 4 * m + r, pos],
                                                    kbd[:, b, n, :], start=False, stop=n == 1 and r == 3)
                last.then_inc(s_done, 1)

            def turn_probs(i):
                pe.wait_ge(p_done, i + 1)
                if i >= 1:
                    pe.wait_ge(pt_read, i)
                for m in range(H // 2):
                    last = nc.tensor.transpose(bank(6 + m // 4)[:, m % 4 * P:(m % 4 + 1) * P],
                                               es[:, i % 2, 2 * m:2 * m + 2, :].rearrange("p h k -> p (h k)"), id32[:])
                last.then_inc(pt_done, 1)

            def values(i):
                pe.wait_ge(pt_read, i + 1)
                if i >= 1:
                    pe.wait_ge(x2_done, i)
                for m in range(H // 2):
                    last = nc.tensor.matmul(bank(1)[:, 0:D], pT[:, i % 2, P * m:P * (m + 1)], vn[:, i // 2, m, :],
                                            start=m == 0, stop=m == H // 2 - 1)
                last.then_inc(o_done, 1)

            pe.wait_ge(qc_read, 2)
            pe.wait_ge(kbd_ready, 1)
            pe.wait_ge(mask_ready, 1)
            for n in range(4):
                rotary(0, n)
            scores(0)
            scores(1)
            pe.wait_ge(fth_ready, 1)
            for b in range(B):
                for e in range(2):
                    if b + 1 < B:
                        rotary(b + 1, 2 * e)
                    turn_probs(2 * b + e)
                    if b + 1 < B:
                        rotary(b + 1, 2 * e + 1)
                    values(2 * b + e)
                if b + 1 < B:
                    scores(2 * b + 2)
                    scores(2 * b + 3)

            for i in range(NT):
                pe.wait_ge(ylo, i + 1)
                for n, part in enumerate((vhi, vlo)):
                    for k in range(KD):
                        c = (n * KD + k) * P
                        last = nc.tensor.transpose(tp[:, i, c:c + P], part[:, i, k * P:(k + 1) * P], id16[:])
                if i % 2:
                    last.then_inc(yt_done, 1)
            for n in range(NC * FJ):
                c, j = divmod(n, FJ)
                pe.wait_ge(yt_read, NT // 2)
                if n >= 2:
                    pe.wait_ge(hid_done, n - 1)
                for m in range(2):
                    for k in range(2 * KD):
                        last = nc.tensor.matmul(bank(2 * (n % 2) + m)[0:rows(j)],
                                                wf16[:, k // 2, F * m + P * j:F * m + P * j + rows(j)],
                                                yT[:, k % 2 * KD + k // 2, CH * c:CH * (c + 1)],
                                                start=k == 0, stop=k == 2 * KD - 1)
                last.then_inc(g_done, 1)
            for i in range(NT):
                c = i // (NT // NC)
                pe.wait_ge(hlo, FJ * (c + 1))
                t = slice(P * (i % (NT // NC)), P * (i % (NT // NC) + 1))
                for j in range(FJ):
                    r = slice(0, rows(j))
                    for n in range(2):
                        last = nc.tensor.matmul(tpf[:, i // 2, (i % 2) * D:(i % 2) * D + D], hid_hl[c][r, n, j, t],
                                                w316[r, j, :], start=j == 0 and n == 0, stop=j == FJ - 1 and n == 1)
                last.then_inc(f_done, 1)


def kernel(**inputs):
    import concourse.bacc as bacc
    import ml_dtypes
    from concourse.bass_utils import run_bass_kernel_spmd

    nc = bacc.Bacc("TRN2", target_bir_lowering=False, num_devices=1)
    a = {k: np.asarray(v) for k, v in inputs.items()}
    def even_odd(v):
        return v.reshape(*v.shape[:-1], D // KD, KD).swapaxes(-1, -2).reshape(v.shape)

    kr = a["L0_xattn_W_kr"]
    kr_swapped = np.concatenate([kr[:, R // 2:], kr[:, :R // 2]], axis=1)
    w3 = even_odd(a["L0_ffn_w3"].T)
    w3 = np.concatenate([w3, np.zeros((FJ * P - F, D), np.float32)]).reshape(FJ, P, D)
    freq = (1.0 / 10000.0 ** (np.arange(R // 2, dtype=np.float32) / (R // 2))).astype(np.float32)
    angle = np.arange(S, dtype=np.float32)[None, :] * freq[:, None]
    cos, sin = np.cos(angle), np.sin(angle)
    ck, sk = cos[:, :LK], sin[:, :LK]
    arrays = {
        "x": even_odd(a["x"]).reshape(T, D),
        "w_attn": even_odd(a["L0_attn_W"].transpose(0, 2, 1)).reshape(L, P, KD, D).transpose(1, 0, 2, 3).reshape(P, L, KD * D),
        "ident16": np.eye(P, dtype=np.float16),
        "ident32": np.eye(P, dtype=np.float32),
        "ctxT": a["ctx_2048"].reshape(B * LK, KD, P).transpose(2, 1, 0),
        "seg": a["itok_BxS_0_1023"].astype(np.int32).reshape(T),
        "w_kvc": a["L0_xattn_W_kvc"].reshape(KD, P, KVC).transpose(1, 0, 2),
        "w_dq": a["L0_xattn_W_dq"].reshape(P, KD, QC),
        "w_uqT": a["L0_xattn_W_uq"].reshape(QC, H // 2, 2, HD).transpose(1, 3, 2, 0),
        "w_qr": a["L0_xattn_W_qr"],
        "w_ukv": np.stack([a[f"L0_xattn_W_{n}"].reshape(KVC, H // 2, 2, HD) for n in ("uk", "uv")]
                          ).transpose(2, 1, 0, 3, 4).reshape(H // 2, KVC, 4, HD),
        "w_kr": np.stack([np.concatenate([kr, kr], axis=1), np.concatenate([kr_swapped, kr_swapped], axis=1)], axis=1),
        "w_o": even_odd(a["L0_xattn_W_o"]).reshape(H, HD, D).transpose(1, 0, 2),
        "w12": np.concatenate([a["L0_ffn_w1"], a["L0_ffn_w2"]]).T.reshape(P, KD, 2 * F),
        "w3": w3.transpose(1, 0, 2),
        "rope_q": np.stack([np.tile(cos, (4, 1)), np.tile(sin, (4, 1))], axis=1),
        "rope_k": np.stack([np.tile(np.concatenate([u, v]), (2, 1)) for u, v in ((ck, ck), (-sk, sk), (ck, -ck), (sk, sk))],
                           axis=1),
        "key_index": -np.arange(LK, dtype=np.float32)[:, None] - LOOKBACK / 2,
        "neg_eye": np.tile(NEG * np.eye(LK), (1, 8)).astype(ml_dtypes.bfloat16),
    }
    arrays = {k: np.ascontiguousarray(v) for k, v in arrays.items()}
    aps = {k: nc.dram_tensor(k, v.shape, mybir.dt.from_np(v.dtype), kind="ExternalInput").ap() for k, v in arrays.items()}
    out = nc.dram_tensor("out", (T, D), F32, kind="ExternalOutput").ap()
    build(nc, out=out, **aps)
    r = run_bass_kernel_spmd(nc, [arrays], core_ids=[0])
    return r.results[0]["out"].reshape(B, S, KD, D // KD).swapaxes(2, 3).reshape(B, S, D)
```

```python
from contextlib import ExitStack

import numpy as np

import concourse.bass as bass
from concourse import mybir

F32 = mybir.dt.float32
F16 = mybir.dt.float16
BF16 = mybir.dt.bfloat16
I32 = mybir.dt.int32
U32 = mybir.dt.uint32
ALU = mybir.AluOpType
ACT = mybir.ActivationFunctionType
AX = mybir.AxisListType

P = 128
B, S, D = 4, 256, 256
T = B * S
NT = T // P
G = 2
GROUPS = NT // G
KD = D // P
L = 8
LK = 64
H, HD, R = 16, 128, 64
QC, KVC = 96, 64
LOOKBACK = 8
F = 704
FJ = (F + P - 1) // P
NEG = -1e30
LN_EPS = 1e-5
Q_EPS = 1e-5
MAGIC = 1.5 * 2.0**23


def build(nc, x, w_attn, ident16, ident32, ctxT, seg, w_kvc, w_dq, w_uqT, w_qr, w_ukv, w_kr, w_o, w12, w3, rope_q, rope_k,
          key_index, neg_eye, out):
    with ExitStack() as ctx:
        def sb(name, shape, dt):
            return ctx.enter_context(nc.sbuf_tensor(name, shape, dt))

        def ps(name, shape, dt):
            return ctx.enter_context(nc.psum_tensor(name, shape, dt))

        def sem(name):
            return ctx.enter_context(nc.semaphore(name))

        xs = sb("xs", [P, NT, D], F32)
        arena_a = sb("arena_a", [P, L * KD * D], F32)
        arena_o = sb("arena_o", [P, H * D], F32)
        arena_u = sb("arena_u", [P, 2 * H * HD], F32)
        stack_w_f32 = arena_a[:, :].rearrange("p (l c) -> p l c", l=L)
        rotary_q = [a[:, :].rearrange("p (n m s) -> p n m s", n=2, s=S) for a in (arena_a, arena_o)]
        wo = arena_o[:, :].rearrange("p (h d) -> p h d", h=H)
        hidden_parts0 = arena_o[:, 0:FJ * 512].bitcast(F16).rearrange("p (n j t) -> p n j t", n=2, j=FJ)
        probs = arena_u[:, 0:2 * H * LK].rearrange("p (n h k) -> p n h k", n=2, h=H)
        probs_T = arena_u[:, 2 * H * LK:4 * H * LK].rearrange("p (n c) -> p n c", n=2)
        arena_k = sb("arena_k", [P, KD * 2 * F + FJ * D], F32)
        wkvc = sb("wkvc", [P, KD, KVC], F32)
        wdq = sb("wdq", [P, KD, QC], F32)
        wqr = sb("wqr", [QC, H * R], F32)
        wkr = sb("wkr", [KVC, 2, 2 * R], F32)
        cos_sin_q = sb("cos_sin_q", [P, 2, S], F32)
        cos_sin_k = sb("cos_sin_k", [P, 4, LK], F32)
        key_middle = sb("key_middle", [LK, 1], F32)
        neg_eye_sb = sb("neg_eye_sb", [LK, 8 * LK], BF16)
        masked = sb("masked", [LK, T], BF16)
        id32 = sb("id32", [P, P], F32)
        kvc = sb("kvc", [KVC, B * LK], F32)
        key_blocks = sb("key_blocks", [P, B, 2, 2 * LK], F32)
        absorbed_keys = sb("absorbed_keys", [QC, B, H, LK], F32)
        absorbed_values = sb("absorbed_values", [P, B, H // 2, D], F32)
        latent_qT = sb("latent_qT", [QC, T], F32)
        smax = sb("smax", [P, 2, H], F32)
        ssum = sb("ssum", [P, 2, H], F32)
        srec = sb("srec", [P, 2, H], F32)
        ff_sums = sb("ff_sums", [P, 4], F32)
        ff_scales = sb("ff_scales", [P, 4], F32)
        ff_upper = sb("ff_upper", [P, 4], F32)
        ff_lower = sb("ff_lower", [P, 4], F32)
        stack_w = sb("stack_w", [P, L, KD, D], F16)
        stack_below = sb("stack_below", [P, KD * D], F16)
        id16 = sb("id16", [P, P], F16)
        ones = sb("ones", [P, P], F32)
        magic = sb("magic", [P, D], F32)
        stack_sums = sb("stack_sums", [P, L], F32)
        stack_scales = sb("stack_scales", [P, L], F32)
        stack_upper = sb("stack_upper", [P, L], F32)
        stack_lower = sb("stack_lower", [P, L], F32)
        stats = sb("stats", [P, NT, 6], F32)
        row_mean_var = sb("row_mean_var", [P, NT, 2], F32)
        rstd = sb("rstd", [P, NT], F32)
        row_var = sb("row_var", [P, NT], F32)
        row_std = sb("row_std", [P, NT], F32)
        normed = sb("normed", [P, NT, D], F32)
        peak_product = sb("peak_product", [P, NT], F32)
        peak_value = sb("peak_value", [P, NT], F32)
        peak_eps = sb("peak_eps", [P, NT], F32)
        peak_recip = sb("peak_recip", [P, NT], F32)
        round_factor = sb("round_factor", [P, NT], F32)
        quant_scale = sb("quant_scale", [P, NT], F32)
        quant_step = sb("quant_step", [P, NT], F32)
        step_mantissa = sb("step_mantissa", [P, NT], F32)
        step_power = sb("step_power", [P, NT], F32)
        product_scale = sb("product_scale", [P, NT], F32)
        above_magic = sb("above_magic", [P, NT, D], F32)
        int_rows = sb("int_rows", [P, NT, D], F16)
        row_high = sb("row_high", [P, NT, D], F16)
        row_low = sb("row_low", [P, NT, D], F16)
        rows_T = sb("rows_T", [P, NT, 4 * P], F16)

        def part(arena, start, *dims):
            size = int(np.prod(dims))
            v = arena[:, start:start + size]
            if len(dims) == 2:
                v = v.rearrange("p (a b) -> p a b", a=dims[0])
            return v

        wukv = part(arena_k, 0, 4, HD)[0:KVC]
        wuqT = part(arena_k, 4 * HD, 2, QC)
        o_k = 4 * HD + 2 * QC
        pair_kvT = part(arena_k, o_k, 2, 2 * B * LK)
        rot_products = part(arena_k, o_k + 4 * B * LK, 4, B * LK)
        raw_rot_keys = part(arena_k, o_k + 8 * B * LK, 2, B * LK)
        ctx_T = part(arena_k, o_k + 10 * B * LK, KD, B * LK)
        ff_w12 = part(arena_k, 0, KD, 2 * F)
        ff_w3 = part(arena_k, KD * 2 * F, FJ, D)
        stack_w_flat = stack_w[:, :, :, :].rearrange("p l k d -> p (l k d)")
        ff_w12_ternary = part(stack_w_flat, 0, KD, 2 * F)
        int_rows_flat = int_rows[:, :, :].rearrange("p i d -> p (i d)")
        ff_w3_ternary = part(int_rows_flat, 0, FJ, D)
        ff_below = above_magic[:, :, :].rearrange("p i d -> p (i d)")[:, 0:FJ * D // 2].bitcast(F16)
        rows_T_flat = rows_T[:, :, :].rearrange("p i c -> p (i c)")
        segs = rows_T_flat[0:LK, 0:2 * T].bitcast(I32)
        seg_distance = above_magic[:, :, :].rearrange("p i d -> p (i d)")[0:LK, 0:T]
        gate_sigmoid = part(arena_u, 0, 2, 512)
        hidden = part(arena_u, 1024, 2, 512)

        acc = ps("acc", [P, NT, D], F32)
        tp = ps("tp", [P, NT, 4 * P], F16)

        accf = acc[:, :, :].rearrange("p i d -> p (i d)").rearrange("p (b c) -> p b c", b=4)
        tpf = tp[:, :, :].rearrange("p i c -> p (i c)").bitcast(F32).rearrange("p (b c) -> p b c", b=4)

        def bank(n):
            return accf[:, n, :] if n < 4 else tpf[:, n - 4, :]

        x_in = sem("x_in")
        stack_w_in = [sem(f"stack_w_in{l}") for l in range(L)]
        id_in = sem("id_in")
        rows_out = sem("rows_out")
        keyside_in = sem("keyside_in")
        ukv_in = sem("ukv_in")
        uq_in = sem("uq_in")
        seg_in = sem("seg_in")
        w_o_in = sem("w_o_in")
        ff_in = sem("ff_in")
        mask_ready = sem("mask_ready")
        queryside_in = sem("queryside_in")
        latent_kv_done = sem("latent_kv_done")
        latent_kv_copied = sem("latent_kv_copied")
        keys_done = sem("keys_done")
        keys_copied = sem("keys_copied")
        values_done = sem("values_done")
        values_copied = sem("values_copied")
        abs_keys_done = sem("abs_keys_done")
        abs_keys_copied = sem("abs_keys_copied")
        abs_values_done = [sem(f"abs_values_done{e}") for e in range(2)]
        abs_values_copied_act = sem("abs_values_copied_act")
        abs_values_copied_dve = sem("abs_values_copied_dve")
        dist_ready = sem("dist_ready")
        rot_in = sem("rot_in")
        krot_zero = sem("krot_zero")
        krot_ready = sem("krot_ready")
        later_std_ready = sem("later_std_ready")
        later_var_ready = sem("later_var_ready")
        queries_normed = sem("queries_normed")
        queriesT_done = sem("queriesT_done")
        queriesT_copied = sem("queriesT_copied")
        latent_done = sem("latent_done")
        latent_copied = sem("latent_copied")
        rotary_done = sem("rotary_done")
        rotary_turned = sem("rotary_turned")
        scores_done = sem("scores_done")
        scores_shifted = sem("scores_shifted")
        exp_done = sem("exp_done")
        recip_done = sem("recip_done")
        probs_done = sem("probs_done")
        probsT_done = sem("probsT_done")
        probsT_copied = sem("probsT_copied")
        attn_done = sem("attn_done")
        attn_added = sem("attn_added")
        ff_thresholds_ready = sem("ff_thresholds_ready")
        ff_sums_ready = sem("ff_sums_ready")
        ff_ternary_ready = sem("ff_ternary_ready")
        ff_totals_ready = sem("ff_totals_ready")
        ff_normed = sem("ff_normed")
        ff_high_ready = sem("ff_high_ready")
        ff_low_ready = sem("ff_low_ready")
        ffT_done = sem("ffT_done")
        ffT_copied = sem("ffT_copied")
        gate_done = sem("gate_done")
        sigmoid_done = sem("sigmoid_done")
        hidden_done = sem("hidden_done")
        hidden_high_done = sem("hidden_high_done")
        hidden_low_done = sem("hidden_low_done")
        result_done = sem("result_done")
        ones_set = sem("ones_set")
        rows_ready = sem("rows_ready")
        stack_sums_ready = sem("stack_sums_ready")
        stack_totals_ready = sem("stack_totals_ready")
        stack_ternary_ready = sem("stack_ternary_ready")
        first_var_ready = sem("first_var_ready")
        first_std_ready = sem("first_std_ready")
        step_done = sem("step_done")
        peaked = sem("peaked")
        r_ready = [sem(f"r_ready{g}") for g in range(GROUPS)]
        rounded = [sem(f"rounded{g}") for g in range(GROUPS)]
        ints_ready = [sem(f"ints_ready{g}") for g in range(GROUPS)]
        step_ready = [sem(f"step_ready{g}") for g in range(GROUPS)]
        hi_ready = [sem(f"hi_ready{g}") for g in range(GROUPS)]
        lo_ready = [sem(f"lo_ready{g}") for g in range(GROUPS)]
        turned = [sem(f"turned{g}") for g in range(GROUPS)]
        turned_copied = [sem(f"turned_copied{g}") for g in range(GROUPS)]
        products_ready = [sem(f"products_ready{g}") for g in range(GROUPS)]

        def before(q, g, d):
            return (q, g - d) if g >= d else (q - 1, g - d + GROUPS)

        half = lambda h: slice(LK * (h % 2), LK * (h % 2) + LK)
        query_rows_T = above_magic[:, :, :].rearrange("p i d -> p (i d)").rearrange("p (k t) -> p k t", k=KD)
        ff_rows_T = rows_T[:, :, :].rearrange("p i c -> p (i c)").rearrange("p (c t) -> p c t", c=2 * KD)
        hidden_parts = [hidden_parts0, arena_a[:, 0:FJ * 512].bitcast(F16).rearrange("p (n j t) -> p n j t", n=2, j=FJ)]
        SCALE = 1.0 / float(np.sqrt(np.float32(HD + R)))
        CH = 512
        NC = T // CH
        rows = lambda j: min(P, F - j * P)

        def value_copies(engine, copy, e, hp, read):
            engine.wait_ge(abs_values_done[e], hp + 1)
            for m in range(2):
                last = copy(absorbed_values[half(e), :, bass.ds(hp, 1), :].rearrange("p (n m) h d -> p m n (h d)", m=2)[:, m],
                            bank(7 - e)[half(m), :].rearrange("p (n d) -> p n d", n=2))
            last.then_inc(read, 1)

        def gate_bank(n, m):
            return bank(2 * ((n + 1) % 2) + m)

        def yt_bank(j):
            if j < 2:
                return accf[:, 0:1, :].bitcast(F16).rearrange("p b (i c) -> p (b i) c", i=2)
            return tp[:, 2 * (j - 2):2 * (j - 2) + 2, :]

        def rotary_bank(k):
            return bank((0, 1, 6, 7, 0, 1)[k] if k < 6 else 0)

        block = ctx.enter_context(nc.Block())

        @block.sync
        def _(sp):
            sp.dma_start(xs[:], x.rearrange("(i p) d -> p i d", p=P)).then_inc(x_in, 16)
            sp.dma_start(wukv, w_ukv[0]).then_inc(ukv_in, 16)
            sp.dma_start(wuqT, w_uqT[0]).then_inc(uq_in, 16)
            for l in range(L):
                sp.dma_start(stack_w_f32[:, l, :], w_attn[:, l, :]).then_inc(stack_w_in[l], 16)
            sp.dma_start(wo, w_o).then_inc(w_o_in, 16)
            with sp.Fori(1, H // 2) as q:
                sp.wait_ge(values_done, q)
                sp.dma_start(wukv, w_ukv[bass.ds(q, 1)].rearrange("a p n c -> p (a n) c")).then_inc(ukv_in, 16)
                sp.wait_ge(abs_keys_done, q)
                sp.dma_start(wuqT, w_uqT[bass.ds(q, 1)].rearrange("a p n c -> p (a n) c")).then_inc(uq_in, 16)
            sp.wait_ge(abs_values_done[1], H // 2)
            sp.wait_ge(krot_ready, 1)
            sp.dma_start(ff_w12, w12).then_inc(ff_in, 16)
            sp.dma_start(ff_w3[:, 0:FJ - 1, :], w3[:, 0:FJ - 1, :]).then_inc(ff_in, 16)
            sp.dma_start(ff_w3[0:F - (FJ - 1) * P, FJ - 1, :], w3[0:F - (FJ - 1) * P, FJ - 1, :]).then_inc(ff_in, 16)
            for i in range(NT):
                sp.wait_ge(rows_ready, i + 1)
                sp.dma_start(out[P * i:P * (i + 1), :], xs[:, i, :]).then_inc(rows_out, 16)
            sp.wait_ge(rows_out, 16 * NT)

        @block.scalar
        def _(act):
            act.dma_start(ctx_T, ctxT).then_inc(keyside_in, 16)
            act.dma_start(wkvc[:], w_kvc).then_inc(keyside_in, 16)
            act.dma_start(wkr[:], w_kr).then_inc(keyside_in, 16)
            act.dma_start(cos_sin_k[:], rope_k).then_inc(keyside_in, 16)
            act.dma_start(segs, seg.partition_broadcast(LK)).then_inc(seg_in, 16)
            act.dma_start(key_middle[:], key_index).then_inc(seg_in, 16)
            act.dma_start(id16[:], ident16).then_inc(id_in, 16)
            act.wait_ge(first_var_ready, 1)
            nc.scalar.activation(row_std[:], row_var[:], ACT.Sqrt).then_inc(first_std_ready, 1)
            for l in range(L // 2):
                act.wait_ge(stack_w_in[l], 16)
                nc.scalar.activation(stack_w[:, l].rearrange("p k d -> p (k d)"), stack_w_f32[:, l, :], ACT.Abs,
                                     accum_out=stack_sums[:, l:l + 1]).then_inc(stack_sums_ready, 1)
            act.wait_ge(seg_in, 32)
            nc.scalar.activation(seg_distance, segs, ACT.Abs, bias=key_middle[:]).then_inc(dist_ready, 1)
            act.wait_ge(latent_kv_done, 1)
            nc.scalar.copy(kvc[:], bank(6)[0:KVC, 0:B * LK]).then_inc(latent_kv_copied, 1)
            act.wait_ge(latent_kv_done, 2)
            nc.scalar.copy(raw_rot_keys.rearrange("p n c -> p (n c)"), bank(7)).then_inc(latent_kv_copied, 1)
            act.dma_start(wdq[:], w_dq).then_inc(queryside_in, 16)
            act.dma_start(wqr[:], w_qr).then_inc(queryside_in, 16)
            act.dma_start(cos_sin_q[:], rope_q).then_inc(queryside_in, 16)
            act.dma_start(id32[:], ident32).then_inc(queryside_in, 16)
            act.dma_start(neg_eye_sb[:], neg_eye).then_inc(queryside_in, 16)
            act.wait_ge(ones_set, 2)

            def round_group(q, g):
                act.wait_ge(r_ready[g], q + 1)
                for i in range(G * g, G * g + G):
                    src = normed if isinstance(q, int) and q == 0 else acc
                    nc.scalar.activation(above_magic[:, i, :], src[:, i, :], ACT.Identity, scale=round_factor[:, i:i + 1],
                                         bias=magic[:, 0:1]).then_inc(rounded[g], 1)

            def high_group(q, g, js=range(G)):
                act.wait_ge(step_ready[g], q + 1)
                for j in js:
                    i = G * g + j
                    act.wait_ge(ints_ready[g], G * q + j + 1)
                    nc.scalar.activation(row_high[:, i, :], int_rows[:, i, :], ACT.Copy, scale=step_mantissa[:, i:i + 1]).then_inc(hi_ready[g], 1)

            def copy_group(q, g):
                act.wait_ge(turned[g], q + 1)
                nc.scalar.copy(rows_T[:, G * g:G * g + G, :].bitcast(U32),
                               tp[:, G * (g % 2):G * (g % 2) + G, :].bitcast(U32)).then_inc(turned_copied[g], 1)

            def key_copies(q, g):
                if g == 0:
                    act.wait_ge(keys_done, q + 1)
                    nc.scalar.copy(pair_kvT[:, 0, :], bank(6)).then_inc(keys_copied, 1)
                elif g == 2:
                    act.wait_ge(abs_keys_done, q + 1)
                    nc.scalar.copy(absorbed_keys[:, :, bass.ds(2 * q, 2), :].rearrange("q b e k -> q e b k"),
                                   bank(6)[0:QC, :].rearrange("q (e b k) -> q e b k", e=2, b=B)).then_inc(abs_keys_copied, 1)
                elif g == 3:
                    value_copies(act, nc.scalar.copy, 1, q, abs_values_copied_act)

            for g in range(GROUPS):
                if g > 0:
                    high_group(*before(0, g, 1))
                if g > 1:
                    copy_group(*before(0, g, 2))
                round_group(0, g)
                key_copies(0, g)
            with act.Fori(1, L) as q:
                for g in range(GROUPS):
                    high_group(*before(q, g, 1), js=[0])
                    copy_group(*before(q, g, 2))
                    high_group(*before(q, g, 1), js=[1])
                    round_group(q, g)
                    key_copies(q, g)
            high_group(L - 1, GROUPS - 1)
            copy_group(L - 1, GROUPS - 2)
            copy_group(L - 1, GROUPS - 1)

            def deviations(n):
                h = slice(NT // 2 * ((n - 1) % 2), NT // 2 * ((n - 1) % 2 + 1))
                act.wait_ge(later_var_ready, n)
                nc.scalar.activation(row_std[:, h], row_var[:, h], ACT.Sqrt).then_inc(later_std_ready, 1)

            deviations(1)
            for c in range(2):
                for j in (2 * c, 2 * c + 1):
                    act.wait_ge(queriesT_done, j + 1)
                    nc.scalar.copy(query_rows_T[:, :, 2 * P * j:2 * P * (j + 1)].rearrange("p k (i t) -> p i k t", i=2),
                                   bank(j).rearrange("p (i k t) -> p i k t", i=2, k=KD)).then_inc(queriesT_copied, 1)
                if c == 0:
                    deviations(2)
                act.wait_ge(latent_done, c + 1)
                nc.scalar.copy(latent_qT[:, 512 * c:512 * (c + 1)], bank(4 + c)[0:QC, :]).then_inc(latent_copied, 1)

            def exps(i):
                act.wait_ge(scores_shifted, i + 1)
                nc.scalar.activation(probs[:, i % 2], probs[:, i % 2], ACT.Exp, scale=SCALE).then_inc(exp_done, 1)

            def copy_probs(i):
                act.wait_ge(probsT_done, i + 1)
                nc.scalar.copy(probs_T[:, i % 2, :], tpf[:, 2:4, :].rearrange("p b c -> p (b c)")).then_inc(probsT_copied, 1)

            def high_rows(tiles):
                for i in tiles:
                    act.wait_ge(ff_normed, i + 1)
                    nc.scalar.copy(row_high[:, i, :], normed[:, i, :]).then_inc(ff_high_ready, 1)

            def copy_rows(j):
                act.wait_ge(ffT_done, j + 1)
                src = yt_bank(j)
                nc.scalar.copy(ff_rows_T[:, :, 2 * P * j:2 * P * (j + 1)].bitcast(U32).rearrange("p c (i t) -> p i c t", i=2),
                               src.bitcast(U32).rearrange("p i (c t) -> p i c t", c=2 * KD)).then_inc(ffT_copied, 1)

            exps(0)
            for i in range(NT):
                copy_probs(i)
                if i + 1 < NT:
                    exps(i + 1)
                if i == 3:
                    deviations(3)
                elif i == 4:
                    high_rows(range(0, 4))
                elif i == 5 or i == 6:
                    copy_rows(i - 5)
            for n in range(NC * FJ):
                c, j = divmod(n, FJ)
                r = slice(0, rows(j))
                if n == 0:
                    deviations(4)
                elif n == 2:
                    high_rows(range(4, 8))
                if n == 5:
                    copy_rows(2)
                    copy_rows(3)
                act.wait_ge(gate_done, n + 1)
                if n >= 2:
                    act.wait_ge(hidden_done, n - 1)
                nc.scalar.activation(gate_sigmoid[r, n % 2, :], gate_bank(n, 0)[r], ACT.Sigmoid, scale=1.0 / 2048).then_inc(sigmoid_done, 1)
                act.wait_ge(hidden_done, n + 1)
                nc.scalar.copy(hidden_parts[c][r, 0, j, :], hidden[r, n % 2, :]).then_inc(hidden_high_done, 1)

        @block.gpsimd
        def _(pool):
            nc.gpsimd.memset(ones[:], 1.0).then_inc(ones_set, 1)
            nc.gpsimd.memset(magic[:], MAGIC).then_inc(ones_set, 1)

            pool.wait_ge(ones_set, 2)

            nc.gpsimd.memset(key_blocks[:], 0.0).then_inc(krot_zero, 1)
            pool.wait_ge(keyside_in, 64)
            pool.wait_ge(latent_kv_copied, 2)
            for n, (src, dst) in enumerate(((0, 0), (1, 1), (1, 2), (0, 3))):
                last = nc.gpsimd.tensor_tensor(rot_products[:, dst, :].rearrange("p (b k) -> p b k", b=B),
                                               raw_rot_keys[:, src, :].rearrange("p (b k) -> p b k", b=B),
                                               cos_sin_k[:, dst:dst + 1, :].to_broadcast([P, B, LK]), ALU.mult)
            last.then_inc(rot_in, 1)
            pool.wait_ge(rot_in, 1)
            pool.wait_ge(krot_zero, 1)
            for n in range(2):
                for e in range(2):
                    last = nc.gpsimd.tensor_tensor(key_blocks[half(e), :, n, half(e)],
                                                   rot_products[half(e), 2 * n, :].rearrange("p (b k) -> p b k", b=B),
                                                   rot_products[half(e), 2 * n + 1, :].rearrange("p (b k) -> p b k", b=B), ALU.add)
            last.then_inc(krot_ready, 1)
            pool.wait_ge(krot_ready, 1)

            def integers(q, g):
                for j in range(G):
                    i = G * g + j
                    pool.wait_ge(rounded[g], G * q + j + 1)
                    nc.gpsimd.tensor_tensor(int_rows[:, i, :], above_magic[:, i, :], magic[:], ALU.subtract).then_inc(ints_ready[g], 1)

            for g in range(GROUPS):
                integers(0, g)
            with pool.Fori(1, L) as q:
                for g in range(GROUPS):
                    integers(q, g)

            def normalize(i):
                pool.wait_ge(recip_done, i + 1)
                nc.gpsimd.tensor_tensor(probs[:, i % 2], probs[:, i % 2], srec[:, i % 2, :].unsqueeze(2).to_broadcast([P, H, LK]),
                                        ALU.mult).then_inc(probs_done, 1)

            for i in range(NT):
                normalize(i)

        @block.vector
        def _(dve):
            done = [0]

            def link(ins):
                done[0] += 1
                ins.then_inc(step_done, 1)
                dve.wait_ge(step_done, done[0])

            dve.wait_ge(x_in, 16)
            for i in range(NT):
                last = nc.vector.bn_stats(stats[:, i, :], xs[:, i, :])
            link(last)
            for i in range(NT):
                last = nc.vector.bn_aggr(row_mean_var[:, i, :], stats[:, i, :])
            link(last)
            nc.vector.tensor_scalar(row_var[:], row_mean_var[:, :, 1], LN_EPS, None, ALU.add).then_inc(first_var_ready, 1)
            dve.wait_ge(first_std_ready, 1)
            dve.wait_ge(first_var_ready, 1)
            link(nc.vector.reciprocal(rstd[:], row_std[:]))
            link(nc.vector.tensor_tensor(row_std[:], rstd[:], rstd[:], ALU.mult))
            link(nc.vector.tensor_tensor(row_std[:], row_std[:], row_var[:], ALU.mult))
            link(nc.vector.tensor_scalar(row_std[:], row_std[:], -0.5, 1.5, ALU.mult, ALU.add))
            link(nc.vector.tensor_tensor(rstd[:], rstd[:], row_std[:], ALU.mult))
            for i in range(NT):
                last = nc.vector.tensor_scalar(normed[:, i, :], xs[:, i, :], row_mean_var[:, i, 0:1], rstd[:, i:i + 1],
                                               ALU.subtract, ALU.mult)
            link(last)
            dve.wait_ge(dist_ready, 1)
            nc.vector.tensor_scalar(masked[:], seg_distance, float(LOOKBACK) / 2, None, ALU.is_gt).then_inc(mask_ready, 1)
            link(nc.vector.tensor_reduce(peak_product[:], normed[:], axis=AX.X, op=ALU.max, apply_absolute_value=True))
            link(nc.vector.tensor_scalar(peak_eps[:], peak_product[:], Q_EPS, None, ALU.add))
            link(nc.vector.reciprocal(peak_recip[:], peak_eps[:]))
            for g in range(GROUPS):
                s = slice(G * g, G * g + G)
                nc.vector.tensor_scalar(round_factor[:, s], peak_recip[:, s], 127.0, None, ALU.mult).then_inc(r_ready[g], 1)
            for g in range(GROUPS):
                dve.wait_ge(r_ready[g], 1)
            link(nc.vector.reciprocal(quant_step[:], round_factor[:]))
            for g in range(GROUPS):
                s = slice(G * g, G * g + G)
                nc.vector.tensor_scalar(step_mantissa[:, s].bitcast(I32), quant_step[:, s].bitcast(I32), 0x7FFFFF, 0x43000000,
                                        ALU.bitwise_and, ALU.bitwise_or).then_inc(step_ready[g], 1)
            link(nc.vector.tensor_scalar(step_power[:].bitcast(I32), quant_step[:].bitcast(I32), 0x7F800000, None, ALU.bitwise_and))
            for l in range(L // 2, L):
                dve.wait_ge(stack_w_in[l], 16)
                nc.vector.tensor_reduce(stack_sums[:, l:l + 1], stack_w_f32[:, l, :], axis=AX.X, op=ALU.add,
                                        apply_absolute_value=True).then_inc(stack_sums_ready, 1)
            dve.wait_ge(stack_totals_ready, 1)
            link(nc.vector.tensor_scalar(stack_scales[:], acc[:, 0, 0:L], 1.0 / (D * D), Q_EPS, ALU.mult, ALU.add))
            nc.vector.tensor_scalar(stack_upper[:], stack_scales[:], 0.5, None, ALU.mult)
            link(nc.vector.tensor_scalar(stack_lower[:], stack_scales[:], -0.5, None, ALU.mult))
            link(nc.vector.tensor_scalar(product_scale[:], step_power[:], 1.0 / 128.0, stack_scales[:, 0:1], ALU.mult, ALU.mult))

            def ternary_layer(l):
                if l > 0:
                    dve.wait_ge(stack_ternary_ready, l)
                link(nc.vector.tensor_scalar(stack_below[:], stack_w_f32[:, l, :], stack_lower[:, l:l + 1], None, ALU.is_lt))
                nc.vector.scalar_tensor_tensor(stack_w[:, l].rearrange("p k d -> p (k d)"), stack_w_f32[:, l, :], stack_upper[:, l:l + 1],
                                               stack_below[:], ALU.is_gt, ALU.subtract).then_inc(stack_ternary_ready, 1)

            def low_tile(q, g, j):
                i = G * g + j
                dve.wait_ge(hi_ready[g], G * q + j + 1)
                nc.vector.scalar_tensor_tensor(row_low[:, i, :], int_rows[:, i, :], step_mantissa[:, i:i + 1], row_high[:, i, :],
                                               ALU.mult, ALU.subtract).then_inc(lo_ready[g], 1)

            def key_copies(q, g):
                if g == 2:
                    dve.wait_ge(values_done, q + 1)
                    nc.vector.tensor_copy(pair_kvT[:, 1, :], bank(7)).then_inc(values_copied, 1)
                elif g == 0:
                    value_copies(dve, nc.vector.tensor_copy, 0, q - 1, abs_values_copied_dve)

            for l in range(2):
                ternary_layer(l)
            for g in range(GROUPS):
                if g > 0:
                    for j in range(G):
                        low_tile(*before(0, g, 1), j)
                if g + 1 < GROUPS:
                    ternary_layer(2 * g + 2)
                    ternary_layer(2 * g + 3)
                if g > 0:
                    key_copies(0, g)
            STEPS = 7

            def peak(q, g):
                s = slice(G * g, G * g + G)
                dve.wait_ge(products_ready[g], q)
                nc.vector.tensor_reduce(peak_product[:, s], acc[:, s, :], axis=AX.X, op=ALU.max,
                                        apply_absolute_value=True).then_inc(peaked, 1)

            def largest(q, g, steps):
                s = slice(G * g, G * g + G)
                dve.wait_ge(peaked, GROUPS * (q - 1) + g + 1)
                nc.vector.tensor_tensor(peak_value[:, s], peak_product[:, s], product_scale[:, s], ALU.mult).then_inc(step_done, steps)

            def scales(q, g, last=False):
                s = slice(G * g, G * g + G)
                start = base + STEPS * (GROUPS * (q - 1) + g)
                following = (q, g + 1) if g + 1 < GROUPS else (q + 1, 0)
                dve.wait_ge(step_done, start - 1)
                nc.vector.tensor_scalar(peak_eps[:, s], peak_value[:, s], Q_EPS, None, ALU.add).then_inc(step_done, 1)
                if not last:
                    peak(*following)
                dve.wait_ge(step_done, start + 1)
                nc.vector.reciprocal(peak_recip[:, s], peak_eps[:, s]).then_inc(step_done, 1)
                dve.wait_ge(step_done, start + 2)
                nc.vector.scalar_tensor_tensor(round_factor[:, s], peak_recip[:, s], 127.0, product_scale[:, s], ALU.mult, ALU.mult).then_inc(r_ready[g], 1)
                nc.vector.tensor_scalar(quant_scale[:, s], peak_recip[:, s], 127.0, None, ALU.mult).then_inc(step_done, 1)
                key_copies(q, g)
                low_tile(*before(q, g, 1), 0)
                dve.wait_ge(step_done, start + 3)
                nc.vector.reciprocal(quant_step[:, s], quant_scale[:, s]).then_inc(step_done, 1)
                low_tile(*before(q, g, 1), 1)
                dve.wait_ge(step_done, start + 4)
                nc.vector.tensor_scalar(step_mantissa[:, s].bitcast(I32), quant_step[:, s].bitcast(I32), 0x7FFFFF, 0x43000000,
                                        ALU.bitwise_and, ALU.bitwise_or).then_inc(step_ready[g], 1)
                nc.vector.tensor_scalar(step_power[:, s].bitcast(I32), quant_step[:, s].bitcast(I32), 0x7F800000, None,
                                        ALU.bitwise_and).then_inc(step_done, 1)
                if not last:
                    largest(*following, 1)
                dve.wait_ge(step_done, start + 5)
                nc.vector.tensor_scalar(product_scale[:, s], step_power[:, s], 1.0 / 128.0, stack_scales[:, bass.ds(q, 1)], ALU.mult,
                                        ALU.mult).then_inc(step_done, 1)

            peak(1, 0)
            largest(1, 0, 2)
            base = done[0] + 2
            with dve.Fori(1, L - 1) as q:
                for g in range(GROUPS):
                    scales(q, g)
            for g in range(GROUPS):
                scales(L - 1, g, last=g == GROUPS - 1)
            for j in range(G):
                low_tile(L - 1, GROUPS - 1, j)
            value_copies(dve, nc.vector.tensor_copy, 0, H // 2 - 1, abs_values_copied_dve)
            done[0] = base + STEPS * GROUPS * (L - 1) - 1
            dve.wait_ge(step_done, done[0])

            def row_statistics(tiles):
                for i in tiles:
                    last = nc.vector.bn_stats(stats[:, i, :], xs[:, i, :])
                link(last)
                for i in tiles:
                    last = nc.vector.bn_aggr(row_mean_var[:, i, :], stats[:, i, :])
                link(last)

            def variances(h):
                nc.vector.tensor_scalar(row_var[:, h], row_mean_var[:, h, 1], LN_EPS, None, ALU.add).then_inc(later_var_ready, 1)

            def norm_scales(h, n, times):
                dve.wait_ge(later_std_ready, n)
                dve.wait_ge(later_var_ready, n)
                link(nc.vector.reciprocal(rstd[:, h], row_std[:, h]))
                link(nc.vector.tensor_tensor(row_std[:, h], rstd[:, h], rstd[:, h], ALU.mult))
                link(nc.vector.tensor_tensor(row_std[:, h], row_std[:, h], row_var[:, h], ALU.mult))
                link(nc.vector.tensor_scalar(row_std[:, h], row_std[:, h], -0.5 * times, 1.5 * times, ALU.mult, ALU.add))
                link(nc.vector.tensor_tensor(rstd[:, h], rstd[:, h], row_std[:, h], ALU.mult))

            def normalized(tiles, ready):
                for i in tiles:
                    nc.vector.tensor_scalar(normed[:, i, :], xs[:, i, :], row_mean_var[:, i, 0:1], rstd[:, i:i + 1],
                                            ALU.subtract, ALU.mult).then_inc(ready, 1)

            halves = [slice(0, NT // 2), slice(NT // 2, NT)]

            def add_stack(h):
                for i in range(NT)[h]:
                    if i % G == 0:
                        dve.wait_ge(products_ready[i // G], L)
                    last = nc.vector.scalar_tensor_tensor(xs[:, i, :], acc[:, i, :], product_scale[:, i:i + 1], xs[:, i, :],
                                                          ALU.mult, ALU.add)
                link(last)

            add_stack(halves[0])
            row_statistics(range(NT)[halves[0]])
            variances(halves[0])
            add_stack(halves[1])
            norm_scales(halves[0], 1, 1.0)
            normalized(range(NT)[halves[0]], queries_normed)
            row_statistics(range(NT)[halves[1]])
            variances(halves[1])
            norm_scales(halves[1], 2, 1.0)
            normalized(range(NT)[halves[1]], queries_normed)

            def feed_forward_sums(n):
                if n == 0:
                    dve.wait_ge(ff_in, 48)
                    link(nc.vector.memset(ff_sums[:], 0.0))
                if n < 2:
                    nc.vector.tensor_reduce(ff_sums[:, n:n + 1], ff_w12[:, :, F * n:F * n + F], axis=AX.XY, op=ALU.add,
                                            apply_absolute_value=True)
                else:
                    nc.vector.tensor_reduce(ff_sums[:, 2:3], ff_w3[:, 0:FJ - 1, :], axis=AX.XY, op=ALU.add,
                                            apply_absolute_value=True)
                    nc.vector.tensor_reduce(ff_sums[0:rows(FJ - 1), 3:4], ff_w3[0:rows(FJ - 1), FJ - 1, :], axis=AX.X,
                                            op=ALU.add, apply_absolute_value=True).then_inc(ff_sums_ready, 1)

            def turn(k):
                b, n = divmod(k, 4)
                dve.wait_ge(rotary_done, k + 1)
                for c in range(2):
                    last = nc.vector.tensor_tensor(rotary_q[b % 2][:, c, 2 * n:2 * n + 2, :],
                                                   rotary_bank(k).rearrange("p (m s) -> p m s", m=2),
                                                   cos_sin_q[:, c:c + 1, :].to_broadcast([P, 2, S]), ALU.mult)
                last.then_inc(rotary_turned, 1)

            def less_max(i):
                src = (accf[:, 2:4, :] if i % 2 == 0 else tpf[:, 0:2, :]).rearrange("p b (h k) -> p (b h) k", k=LK)
                dve.wait_ge(scores_done, i + 1)
                if i >= 2:
                    dve.wait_ge(probsT_done, i - 1)
                link(nc.vector.tensor_reduce(smax[:, i % 2, :], src, axis=AX.X, op=ALU.max))
                nc.vector.tensor_tensor(probs[:, i % 2], src, smax[:, i % 2, :].unsqueeze(2).to_broadcast([P, H, LK]),
                                        ALU.subtract).then_inc(scores_shifted, 1)

            def sums(i):
                dve.wait_ge(exp_done, i + 1)
                link(nc.vector.tensor_reduce(ssum[:, i % 2, :], probs[:, i % 2], axis=AX.X, op=ALU.add))
                nc.vector.reciprocal(srec[:, i % 2, :], ssum[:, i % 2, :]).then_inc(recip_done, 1)

            def add_attn(i):
                dve.wait_ge(attn_done, i + 1)
                nc.vector.tensor_tensor(xs[:, i, :], bank(1)[:, 0:D], xs[:, i, :], ALU.add).then_inc(attn_added, 1)

            def feed_forward_thresholds():
                dve.wait_ge(ff_totals_ready, 1)
                link(nc.vector.tensor_scalar(ff_scales[:, 0:2], bank(0)[:, 0:2], 1.0 / (F * D), 1e-8, ALU.mult, ALU.add))
                link(nc.vector.tensor_reduce(ff_sums[:, 0:1], bank(0)[:, 2:4], axis=AX.X, op=ALU.add))
                link(nc.vector.tensor_scalar(ff_scales[:, 2:3], ff_sums[:, 0:1], 1.0 / (F * D), 1e-8, ALU.mult, ALU.add))
                nc.vector.tensor_scalar(ff_upper[:, 0:3], ff_scales[:, 0:3], 0.5, None, ALU.mult)
                nc.vector.tensor_scalar(ff_lower[:, 0:3], ff_scales[:, 0:3], -0.5, None, ALU.mult).then_inc(ff_thresholds_ready, 1)
                dve.wait_ge(ff_thresholds_ready, 1)

            def low_rows(tiles):
                for i in tiles:
                    dve.wait_ge(ff_high_ready, i + 1)
                    nc.vector.tensor_tensor(row_low[:, i, :], normed[:, i, :], row_high[:, i, :], ALU.subtract).then_inc(ff_low_ready, 1)

            def ternary(n):
                if n < 2 * KD:
                    k, m = divmod(n, 2)
                    w, o, th = ff_w12[:, k, F * m:F * m + F], ff_w12_ternary[:, k, F * m:F * m + F], m
                    tmp = ff_below[:, 0:F]
                elif n == 2 * KD:
                    w, o, th = ff_w3[:, 0:FJ - 1, :], ff_w3_ternary[:, 0:FJ - 1, :], 2
                    tmp = ff_below[:, 0:(FJ - 1) * D].rearrange("p (j d) -> p j d", j=FJ - 1)
                else:
                    r = slice(0, rows(FJ - 1))
                    w, o, th = ff_w3[r, FJ - 1, :], ff_w3_ternary[r, FJ - 1, :], 2
                    tmp = ff_below[r, 0:D]
                q = slice(0, w.shape[0])
                link(nc.vector.tensor_scalar(tmp, w, ff_lower[q, th:th + 1], None, ALU.is_lt))
                nc.vector.scalar_tensor_tensor(o, w, ff_upper[q, th:th + 1], tmp, ALU.is_gt, ALU.subtract).then_inc(ff_ternary_ready, 1)
                dve.wait_ge(ff_ternary_ready, n + 1)

            dve.wait_ge(queryside_in, 80)
            for k in range(6):
                turn(k)
                if k == 4:
                    less_max(0)
            sums(0)
            for i in range(NT):
                if 6 + 2 * i < 4 * B:
                    turn(6 + 2 * i)
                if i + 1 < NT:
                    less_max(i + 1)
                if 6 + 2 * i < 4 * B:
                    turn(7 + 2 * i)
                if i + 1 < NT:
                    sums(i + 1)
                if i == 4:
                    norm_scales(halves[0], 3, 2048.0)
                    normalized(range(NT)[halves[0]], ff_normed)
                elif i == 5:
                    feed_forward_thresholds()
                    low_rows(range(NT)[halves[0]])
                    ternary(0)
                    ternary(1)
                elif i == 6:
                    ternary(2)
                    ternary(3)
                add_attn(i)
                if i < 3:
                    feed_forward_sums(i)
                elif i == 3:
                    dve.wait_ge(attn_added, 4)
                    row_statistics(range(NT)[halves[0]])
                    variances(halves[0])
            dve.wait_ge(attn_added, NT)
            row_statistics(range(NT)[halves[1]])
            variances(halves[1])

            def low(n):
                c, j = divmod(n, FJ)
                r = slice(0, rows(j))
                dve.wait_ge(hidden_high_done, n + 1)
                nc.vector.tensor_tensor(hidden_parts[c][r, 1, j, :], hidden[r, n % 2, :], hidden_parts[c][r, 0, j, :],
                                        ALU.subtract).then_inc(hidden_low_done, 1)

            for n in range(NC * FJ):
                c, j = divmod(n, FJ)
                r = slice(0, rows(j))
                if n == 1:
                    norm_scales(halves[1], 4, 2048.0)
                    normalized(range(NT)[halves[1]], ff_normed)
                if n == 2:
                    low_rows(range(NT)[halves[1]])
                if n in (6, 8):
                    ternary(4 if n == 6 else 5)
                dve.wait_ge(sigmoid_done, n + 1)
                if n >= 2:
                    dve.wait_ge(hidden_low_done, n - 1)
                nc.vector.scalar_tensor_tensor(hidden[r, n % 2, :], gate_bank(n, 1)[r], 1.0 / 16, gate_sigmoid[r, n % 2, :],
                                               ALU.mult, ALU.mult).then_inc(hidden_done, 1)
                if n >= 1:
                    low(n - 1)
            low(NC * FJ - 1)
            for i in range(NT):
                if i % 2 == 0:
                    dve.wait_ge(result_done, i + 2)
                nc.vector.scalar_tensor_tensor(xs[:, i, :], tpf[:, i // 2, (i % 2) * D:(i % 2) * D + D], 1.0 / 128,
                                               xs[:, i, :], ALU.mult, ALU.add).then_inc(rows_ready, 1)

        @block.tensor
        def _(pe):
            pe.wait_ge(keyside_in, 64)
            for k in range(KD):
                last = nc.tensor.matmul(bank(6)[0:KVC, 0:B * LK], wkvc[:, k, :], ctx_T[:, k, :], start=k == 0, stop=k == KD - 1)
            last.then_inc(latent_kv_done, 1)
            pe.wait_ge(latent_kv_copied, 1)
            for m in range(2):
                last = nc.tensor.matmul(bank(7)[:, B * LK * m:B * LK * (m + 1)], wkr[:, m, :], kvc[:], start=True, stop=True)
            last.then_inc(latent_kv_done, 1)
            pe.wait_ge(ones_set, 1)
            pe.wait_ge(stack_sums_ready, L)
            nc.tensor.matmul(acc[:, 0, 0:L], ones[:], stack_sums[:], start=True, stop=True).then_inc(stack_totals_ready, 1)
            pe.wait_ge(id_in, 16)

            def turn_group(q, g, first=False):
                if not first:
                    pe.wait_ge(turned_copied[(g - 2) % GROUPS], q + 1 if g >= 2 else q)
                for j in range(G):
                    i = G * g + j
                    pe.wait_ge(lo_ready[g], G * q + j + 1)
                    for n, half_of in enumerate((row_low, row_high)):
                        for k in range(KD):
                            c = (k * 2 + n) * P
                            last = nc.tensor.transpose(tp[:, G * (g % 2) + j, c:c + P], half_of[:, i, k * P:(k + 1) * P],
                                                       id16[:])
                last.then_inc(turned[g], 1)

            def multiply_group(q, g):
                pe.wait_ge(turned_copied[g], q + 1)
                if g == 0:
                    pe.wait_ge(stack_ternary_ready, q + 1)
                for i in range(G * g, G * g + G):
                    for n in range(2 * KD):
                        w = stack_w[:, bass.ds(q, 1), n // 2, :].rearrange("p a d -> p (a d)")
                        last = nc.tensor.matmul(acc[:, i, :], rows_T[:, i, n * P:(n + 1) * P], w, start=n == 0,
                                                stop=n == 2 * KD - 1)
                last.then_inc(products_ready[g], 1)

            def key_products(q, g, first=False):
                bkt = B * LK
                if g == 0:
                    pe.wait_ge(ukv_in, 16 * q + 16)
                    if not first:
                        pe.wait_ge(abs_values_copied_act, q)
                    for e in range(2):
                        last = nc.tensor.matmul(bank(6)[:, bkt * e:bkt * (e + 1)], wukv[:, e, :], kvc[:],
                                                start=True, stop=True)
                    last.then_inc(keys_done, 1)
                elif g == 1:
                    if first:
                        pe.wait_ge(latent_kv_copied, 2)
                    else:
                        pe.wait_ge(abs_values_copied_dve, q)
                    for e in range(2):
                        last = nc.tensor.matmul(bank(7)[:, bkt * e:bkt * (e + 1)], wukv[:, 2 + e, :], kvc[:],
                                                start=True, stop=True)
                    last.then_inc(values_done, 1)
                elif g == 2:
                    pe.wait_ge(keys_copied, q + 1)
                    pe.wait_ge(uq_in, 16 * q + 16)
                    for e in range(2):
                        last = nc.tensor.matmul(bank(6)[0:QC, bkt * e:bkt * (e + 1)], wuqT[:, e, :], pair_kvT[:, 0, bkt * e:bkt * (e + 1)],
                                                start=True, stop=True)
                    last.then_inc(abs_keys_done, 1)
                else:
                    if first:
                        pe.wait_ge(w_o_in, 16)
                    for e in range(2):
                        pe.wait_ge(*((values_copied, q + 1) if e == 0 else (abs_keys_copied, q + 1)))
                        for m in range(2):
                            o = bkt * e + 2 * LK * m
                            w = wo[:, bass.ds(2 * q + e, 1), :].rearrange("p a d -> p (a d)")
                            last = nc.tensor.matmul(bank(7 - e)[:, D * m:D * (m + 1)], pair_kvT[:, 1, o:o + 2 * LK], w,
                                                    start=True, stop=True)
                        last.then_inc(abs_values_done[e], 1)

            for g in range(GROUPS):
                if g >= 2:
                    multiply_group(*before(0, g, 2))
                key_products(0, g, first=True)
                if g >= 1:
                    turn_group(*before(0, g, 1), first=g < 3)
            with pe.Fori(1, L) as q:
                for g in range(GROUPS):
                    key_products(q, g)
                    multiply_group(*before(q, g, 2))
                    turn_group(*before(q, g, 1))
            multiply_group(L - 1, GROUPS - 2)
            turn_group(L - 1, GROUPS - 1)
            multiply_group(L - 1, GROUPS - 1)

            pe.wait_ge(queryside_in, 80)
            def turn_rows(c):
                for i in range(4 * c, 4 * c + 4):
                    pe.wait_ge(queries_normed, i + 1)
                    for k in range(KD):
                        o = (i % 2 * KD + k) * P
                        last = nc.tensor.transpose(bank(i // 2)[:, o:o + P], normed[:, i, k * P:(k + 1) * P], id32[:])
                    if i % 2:
                        last.then_inc(queriesT_done, 1)

            def latent_queries(c):
                pe.wait_ge(queriesT_copied, 2 * c + 2)
                for k in range(KD):
                    last = nc.tensor.matmul(bank(4 + c)[0:QC, :], wdq[:, k, :], query_rows_T[:, k, 512 * c:512 * (c + 1)],
                                            start=k == 0, stop=k == KD - 1)
                last.then_inc(latent_done, 1)

            def rotary(k):
                b, n = divmod(k, 4)
                free = 0 if k < 4 else k - 3 if k < 6 else k - 1 if k == 6 else k
                if free > 0:
                    pe.wait_ge(rotary_turned, free)
                for e in range(2):
                    m = 2 * n + e
                    last = nc.tensor.matmul(rotary_bank(k)[:, S * e:S * (e + 1)], wqr[:, 2 * R * m:2 * R * (m + 1)],
                                            latent_qT[:, S * b:S * (b + 1)], start=True, stop=True)
                last.then_inc(rotary_done, 1)

            def scores(i):
                b = i // 2
                tok = slice(P * i, P * (i + 1))
                pos = slice(P * (i % 2), P * (i % 2 + 1))
                pe.wait_ge(rotary_turned, 4 * b + 4)
                if i >= 2:
                    pe.wait_ge(scores_shifted, i - 1)
                for m in range(2):
                    dst = bank(2 + 2 * (i % 2) + m)
                    nc.tensor.matmul(dst, latent_qT[:, tok], absorbed_keys[:, b, 8 * m:8 * m + 8, :].rearrange("q h k -> q (h k)"),
                                     start=True, stop=False)
                    nc.tensor.matmul(dst, masked[:, tok], neg_eye_sb[:], start=False, stop=False)
                    for r in range(4):
                        for n in range(2):
                            last = nc.tensor.matmul(dst[:, 2 * LK * r:2 * LK * (r + 1)], rotary_q[b % 2][:, n, 4 * m + r, pos],
                                                    key_blocks[:, b, n, :], start=False, stop=n == 1 and r == 3)
                last.then_inc(scores_done, 1)

            def turn_norms(j):
                for i in (2 * j, 2 * j + 1):
                    pe.wait_ge(ff_low_ready, i + 1)
                    for n, half_of in enumerate((row_high, row_low)):
                        for k in range(KD):
                            o = (n * KD + k) * P
                            last = nc.tensor.transpose(yt_bank(j)[:, i % 2, o:o + P], half_of[:, i, k * P:(k + 1) * P],
                                                       id16[:])
                last.then_inc(ffT_done, 1)

            def gate_products(n):
                c, j = divmod(n, FJ)
                if n == 0:
                    pe.wait_ge(ff_ternary_ready, 2 * KD)
                elif n == 1:
                    pe.wait_ge(attn_added, NT)
                pe.wait_ge(ffT_copied, NT // 4 * (c + 1))
                if n >= 2:
                    pe.wait_ge(hidden_done, n - 1)
                for m in range(2):
                    for k in range(2 * KD):
                        last = nc.tensor.matmul(gate_bank(n, m)[0:rows(j)],
                                                ff_w12_ternary[:, k // 2, F * m + P * j:F * m + P * j + rows(j)],
                                                ff_rows_T[:, k % 2 * KD + k // 2, CH * c:CH * (c + 1)],
                                                start=k == 0, stop=k == 2 * KD - 1)
                last.then_inc(gate_done, 1)

            def turn_probs(i):
                pe.wait_ge(probs_done, i + 1)
                if i >= 1:
                    pe.wait_ge(probsT_copied, i)
                for m in range(H // 2):
                    last = nc.tensor.transpose(bank(6 + m // 4)[:, m % 4 * P:(m % 4 + 1) * P],
                                               probs[:, i % 2, 2 * m:2 * m + 2, :].rearrange("p h k -> p (h k)"), id32[:])
                last.then_inc(probsT_done, 1)

            def values(i):
                pe.wait_ge(probsT_copied, i + 1)
                if i >= 1:
                    pe.wait_ge(attn_added, i)
                for m in range(H // 2):
                    last = nc.tensor.matmul(bank(1)[:, 0:D], probs_T[:, i % 2, P * m:P * (m + 1)], absorbed_values[:, i // 2, m, :],
                                            start=m == 0, stop=m == H // 2 - 1)
                last.then_inc(attn_done, 1)

            turn_rows(0)
            latent_queries(0)
            turn_rows(1)
            pe.wait_ge(abs_values_copied_act, H // 2)
            pe.wait_ge(abs_values_copied_dve, H // 2)
            pe.wait_ge(latent_copied, 1)
            for k in range(4):
                rotary(k)
            latent_queries(1)
            pe.wait_ge(latent_copied, 2)
            pe.wait_ge(krot_ready, 1)
            pe.wait_ge(mask_ready, 1)
            scores(0)
            rotary(4)
            rotary(5)
            for i in range(NT):
                if i == 5:
                    pe.wait_ge(rotary_turned, 4 * B)
                    pe.wait_ge(ff_sums_ready, 1)
                    nc.tensor.matmul(bank(0)[:, 0:4], ones[:], ff_sums[:], start=True, stop=True).then_inc(ff_totals_ready, 1)
                if i + 1 < NT:
                    scores(i + 1)
                if i == 6:
                    pe.wait_ge(ff_thresholds_ready, 1)
                    turn_norms(0)
                elif i == 7:
                    pe.wait_ge(ffT_copied, 1)
                    turn_norms(1)
                if 6 + 2 * i < 4 * B:
                    rotary(6 + 2 * i)
                turn_probs(i)
                if 6 + 2 * i < 4 * B:
                    rotary(7 + 2 * i)
                values(i)

            for n in range(NC * FJ):
                if n == 4:
                    turn_norms(2)
                    turn_norms(3)
                gate_products(n)
            for i in range(NT):
                c = i // (NT // NC)
                if i == 0:
                    pe.wait_ge(ff_ternary_ready, 6)
                pe.wait_ge(hidden_low_done, FJ * (c + 1))
                t = slice(P * (i % (NT // NC)), P * (i % (NT // NC) + 1))
                for j in range(FJ):
                    r = slice(0, rows(j))
                    for n in range(2):
                        last = nc.tensor.matmul(tpf[:, i // 2, (i % 2) * D:(i % 2) * D + D], hidden_parts[c][r, n, j, t],
                                                ff_w3_ternary[r, j, :], start=j == 0 and n == 0, stop=j == FJ - 1 and n == 1)
                last.then_inc(result_done, 1)


def kernel(**inputs):
    import concourse.bacc as bacc
    import ml_dtypes
    from concourse.bass_utils import run_bass_kernel_spmd

    nc = bacc.Bacc("TRN2", target_bir_lowering=False, num_devices=1)
    a = {k: np.asarray(v) for k, v in inputs.items()}
    def even_odd(v):
        return v.reshape(*v.shape[:-1], D // KD, KD).swapaxes(-1, -2).reshape(v.shape)

    kr = a["L0_xattn_W_kr"]
    kr_swapped = np.concatenate([kr[:, R // 2:], kr[:, :R // 2]], axis=1)
    w3 = even_odd(a["L0_ffn_w3"].T)
    w3 = np.concatenate([w3, np.zeros((FJ * P - F, D), np.float32)]).reshape(FJ, P, D)
    freq = (1.0 / 10000.0 ** (np.arange(R // 2, dtype=np.float32) / (R // 2))).astype(np.float32)
    angle = np.arange(S, dtype=np.float32)[None, :] * freq[:, None]
    cos, sin = np.cos(angle), np.sin(angle)
    ck, sk = cos[:, :LK], sin[:, :LK]
    arrays = {
        "x": even_odd(a["x"]).reshape(T, D),
        "w_attn": even_odd(a["L0_attn_W"].transpose(0, 2, 1)).reshape(L, P, KD, D).transpose(1, 0, 2, 3).reshape(P, L, KD * D),
        "ident16": np.eye(P, dtype=np.float16),
        "ident32": np.eye(P, dtype=np.float32),
        "ctxT": a["ctx_2048"].reshape(B * LK, KD, P).transpose(2, 1, 0),
        "seg": a["itok_BxS_0_1023"].astype(np.int32).reshape(T),
        "w_kvc": a["L0_xattn_W_kvc"].reshape(KD, P, KVC).transpose(1, 0, 2),
        "w_dq": a["L0_xattn_W_dq"].reshape(P, KD, QC),
        "w_uqT": a["L0_xattn_W_uq"].reshape(QC, H // 2, 2, HD).transpose(1, 3, 2, 0),
        "w_qr": a["L0_xattn_W_qr"],
        "w_ukv": np.stack([a[f"L0_xattn_W_{n}"].reshape(KVC, H // 2, 2, HD) for n in ("uk", "uv")]
                          ).transpose(2, 1, 0, 3, 4).reshape(H // 2, KVC, 4, HD),
        "w_kr": np.stack([np.concatenate([kr, kr], axis=1), np.concatenate([kr_swapped, kr_swapped], axis=1)], axis=1),
        "w_o": even_odd(a["L0_xattn_W_o"]).reshape(H, HD, D).transpose(1, 0, 2),
        "w12": np.concatenate([a["L0_ffn_w1"], a["L0_ffn_w2"]]).T.reshape(P, KD, 2 * F),
        "w3": w3.transpose(1, 0, 2),
        "rope_q": np.stack([np.tile(cos, (4, 1)), np.tile(sin, (4, 1))], axis=1),
        "rope_k": np.stack([np.tile(np.concatenate([u, v]), (2, 1)) for u, v in ((ck, ck), (-sk, sk), (ck, -ck), (sk, sk))],
                           axis=1),
        "key_index": -np.arange(LK, dtype=np.float32)[:, None] - LOOKBACK / 2,
        "neg_eye": np.tile(NEG * np.eye(LK), (1, 8)).astype(ml_dtypes.bfloat16),
    }
    arrays = {k: np.ascontiguousarray(v) for k, v in arrays.items()}
    aps = {k: nc.dram_tensor(k, v.shape, mybir.dt.from_np(v.dtype), kind="ExternalInput").ap() for k, v in arrays.items()}
    out = nc.dram_tensor("out", (T, D), F32, kind="ExternalOutput").ap()
    build(nc, out=out, **aps)
    r = run_bass_kernel_spmd(nc, [arrays], core_ids=[0])
    return r.results[0]["out"].reshape(B, S, KD, D // KD).swapaxes(2, 3).reshape(B, S, D)
```
